# Optimizing a Trainium2 kernel written in Bass

```python
import numpy as np
import jax
import jax.numpy as jnp

def _softmax(x, axis=-1):
    return jax.nn.softmax(x, axis=axis)

def _gelu(x):
    return jax.nn.gelu(x, approximate=True)

def _silu(x):
    return jax.nn.silu(x)

def _sigmoid(x):
    return jax.nn.sigmoid(x)

def _layernorm(x, axis=-1, eps=1e-05):
    m = jnp.mean(x, axis=axis, keepdims=True)
    v = jnp.var(x, axis=axis, keepdims=True)
    return (x - m) / jnp.sqrt(v + eps)

def _scatter_add(tgt, idx, src, axis=0):
    return tgt.at[idx].add(src)

def _segment_sum(src, seg, n):
    return jax.ops.segment_sum(src, seg, n)
kernel_name = 'mk_gnn_resnorm_d1_gnn_r32_992402'

def setup_inputs(seed: int=0):
    np.random.seed(seed)
    _w = jnp.asarray

    def _rec_inputs():
        import jax
        import jax.numpy as jnp
        _gk = jax.random.key(seed)
        x = -0.0005121 + 1.001 * jax.random.normal(jax.random.fold_in(_gk, 1), (50000, 64), jnp.float32)
        src = jax.random.randint(jax.random.fold_in(_gk, 2), (50000,), 0, 50000, jnp.int32)
        dst = jax.random.randint(jax.random.fold_in(_gk, 3), (50000,), 0, 50000, jnp.int32)
        _o = jnp.argsort(dst, stable=True)
        src = src[_o]
        dst = dst[_o]
        edge_attr_64 = -9.77346e-05 + 0.999888 * jax.random.normal(jax.random.fold_in(_gk, 12), (50000, 64), jnp.float32)
        return (x, src, dst, edge_attr_64)
    x, src, dst, edge_attr_64 = _rec_inputs()

    def _L0_gnn_setup():
        import jax, jax.numpy as jnp
        import numpy as np
        N, E, DN, DE, H = (50000, 25000, 64, 64, 128)
        key = jax.random.key(seed)
        ks = jax.random.split(key, 12)
        s = 0.05
        return {'h': jax.random.normal(ks[0], (N, DN), jnp.float32), 'eh': jax.random.normal(ks[1], (E, DE), jnp.float32), 'W_node1': jax.random.normal(ks[2], (DN, H), jnp.float32) * s, 'b_node1': jax.random.normal(ks[3], (H,), jnp.float32) * s, 'W_node2': jax.random.normal(ks[4], (H, H), jnp.float32) * s, 'W_edge1': jax.random.normal(ks[5], (DE, H), jnp.float32) * s, 'b_edge1': jax.random.normal(ks[6], (H,), jnp.float32) * s, 'W_edge2': jax.random.normal(ks[7], (H, H), jnp.float32) * s, 'W_comb': jax.random.normal(ks[8], (H, DN), jnp.float32) * s, 'W_ue': jax.random.normal(ks[9], (DN, DE), jnp.float32) * s, 'src': jax.random.randint(ks[10], (E,), 0, N, jnp.int32), 'dst': jax.random.randint(ks[11], (E,), 0, N, jnp.int32)}
    _L0_gnn_all = _L0_gnn_setup()
    _L0_gnn_in = {k: v for k, v in _L0_gnn_all.items() if k in ('W_node1', 'b_node1', 'W_node2', 'W_edge1', 'b_edge1', 'W_edge2', 'W_comb', 'W_ue')}
    del _L0_gnn_all
    return {'x': x, 'src': src, 'dst': dst, 'edge_attr_64': edge_attr_64, 'L0_gnn_W_node1': _L0_gnn_in['W_node1'], 'L0_gnn_b_node1': _L0_gnn_in['b_node1'], 'L0_gnn_W_node2': _L0_gnn_in['W_node2'], 'L0_gnn_W_edge1': _L0_gnn_in['W_edge1'], 'L0_gnn_b_edge1': _L0_gnn_in['b_edge1'], 'L0_gnn_W_edge2': _L0_gnn_in['W_edge2'], 'L0_gnn_W_comb': _L0_gnn_in['W_comb'], 'L0_gnn_W_ue': _L0_gnn_in['W_ue']}

def reference(x, src, dst, edge_attr_64, L0_gnn_W_node1, L0_gnn_b_node1, L0_gnn_W_node2, L0_gnn_W_edge1, L0_gnn_b_edge1, L0_gnn_W_edge2, L0_gnn_W_comb, L0_gnn_W_ue):
    import jax
    import jax.numpy as jnp

    def _L0_gnn_ref(h, eh, W_node1, b_node1, W_node2, W_edge1, b_edge1, W_edge2, W_comb, W_ue, src, dst):
        import jax, jax.numpy as jnp
        import numpy as np
        N, E, DN, DE, H = (50000, 25000, 64, 64, 128)
        hs = h[src]
        hd = h[dst]
        eh_new = 0.8 * eh + 0.2 * (hs * hd @ W_ue)
        m1 = jax.nn.relu(hs @ W_node1 + b_node1) @ W_node2
        m2 = jax.nn.relu(eh_new @ W_edge1 + b_edge1) @ W_edge2
        m = jnp.tanh(m1 * m2 @ W_comb)
        agg = jax.ops.segment_sum(m, dst, num_segments=h.shape[0])
        return agg + h
    x = _layernorm(x + _L0_gnn_ref(x, edge_attr_64, L0_gnn_W_node1, L0_gnn_b_node1, L0_gnn_W_node2, L0_gnn_W_edge1, L0_gnn_b_edge1, L0_gnn_W_edge2, L0_gnn_W_comb, L0_gnn_W_ue, src, dst), axis=-1)
    return x

_drawn_inputs = setup_inputs


def setup_inputs(seed=0):
    import zlib

    import numpy as np

    out = dict(_drawn_inputs(seed))
    spreads = {}
    factors = {'edge_attr_64': 8.0,
     'L0_gnn_W_node1': 8.0,
     'L0_gnn_b_node1': 8.0,
     'L0_gnn_W_node2': 8.0,
     'L0_gnn_W_edge1': 8.0,
     'L0_gnn_b_edge1': 8.0,
     'L0_gnn_W_edge2': 8.0,
     'L0_gnn_W_comb': 8.0,
     'L0_gnn_W_ue': 8.0}
    for name, (base, spread) in spreads.items():
        noise = np.random.default_rng([zlib.crc32(name.encode()), seed]).standard_normal(out[name].shape)
        drawn = base * np.exp(spread * noise) if base else spread * noise
        out[name] = jnp.asarray(drawn.astype(out[name].dtype))
    for name, factor in factors.items():
        out[name] = (out[name] * factor).astype(out[name].dtype)
    return out
```

```python
from contextlib import ExitStack

import concourse.bass as bass
from concourse import mybir

P = 128
F32 = mybir.dt.float32
I32 = mybir.dt.int32
ALU = mybir.AluOpType
ACT = mybir.ActivationFunctionType
AX_X = mybir.AxisListType.X

TPG = 4
NB = 2
LN_BLOCKS = 23


def gnn_kernel(nc, x, src, dst, eh, w_n1, b_n1, w_n2, w_e1, b_e1, w_e2, w_comb, w_ue, out):
    N, D = x.shape
    E = src.shape[0]
    H = w_n1.shape[1]
    G = -(-E // (P * TPG))
    T = G * TPG
    GE = P * TPG
    FULL_T = E // P
    TAIL_E = E - FULL_T * P
    CH = -(-T // P)
    TAIL_T = T - (CH - 1) * P
    B = -(-N // P)
    TAIL_N = N - (B - 1) * P
    LC = B // LN_BLOCKS
    assert LC * LN_BLOCKS == B and G % NB == 0 and D == 64 and H == P
    LW = LN_BLOCKS * D

    with ExitStack() as ctx:
        def sb(name, shape, dt=F32):
            return ctx.enter_context(nc.sbuf_tensor(name, shape, dt))

        def ps(name, shape, dt=F32):
            return ctx.enter_context(nc.psum_tensor(name, shape, dt))

        def sem(name):
            return ctx.enter_context(nc.semaphore(name))

        dst_rows = nc.dram_tensor("dst_rows", (T, P), F32, kind="Internal").ap()
        sums = nc.dram_tensor("node_sums", (N + P, D), F32, kind="Internal").ap()

        ident = sb("ident", [P, P])
        lower = sb("lower", [P, P])
        w1 = sb("w1", [D, H])
        w2 = sb("w2", [H, H])
        we = sb("we", [P, H])
        we1_low = sb("we1_low", [D, H])
        we2 = sb("we2", [H, H])
        wc = sb("wc", [H, D])
        wue = sb("wue", [D, D])
        wueT = sb("wueT", [D, D])
        b1 = sb("b1", [H, 1])
        be1 = sb("be1", [H, 1])
        eps = sb("eps", [P, 1])
        raw = sb("raw", [P, 2, CH, P], I32)
        rawf = sb("rawf", [P, 2, CH, P])
        idx = sb("idx", [P, G, 2 * TPG], I32)
        dstf = sb("dstf", [P, T])
        spare = sb("spare", [P, T])
        idx_now = sb("idx_now", [P, NB, 2 * TPG], I32)
        nodes = sb("nodes", [P, B * D])
        xin = sb("xin", [P, NB, TPG, 2 * D])
        hd = sb("hd", [P, NB, TPG, D])
        dst_all = sb("dst_all", [P, NB, GE])
        hsT = sb("hsT", [D, GE])
        peT = sb("peT", [P, GE])
        r1 = sb("r1", [H, GE])
        r2 = sb("r2", [H, GE])
        m1 = sb("m1", [H, GE])
        m12 = sb("m12", [H, GE])
        msg = sb("msg", [P, TPG, D])
        same = sb("same", [P, 2, TPG, P])
        junk = sb("junk", [P, TPG, P])
        earlier = sb("earlier", [P, TPG])
        dup = sb("dup", [P, TPG])
        moved = sb("moved", [P, TPG])
        put_at = sb("put_at", [P, 2, TPG], I32)
        tot = sb("tot", [P, 2, TPG, D])
        sq = sb("sq", [P, 2, LW])
        mean = sb("mean", [P, 2, LN_BLOCKS])
        nmean = sb("nmean", [P, 2, LN_BLOCKS])
        ssq = sb("ssq", [P, 2, LN_BLOCKS])
        std = sb("std", [P, 2, LN_BLOCKS])
        rstd = sb("rstd", [P, 2, LN_BLOCKS])

        psT = ps("psT", [P, GE])
        psH = ps("psH", [P, GE])
        psA = ps("psA", [P, GE])
        psB = ps("psB", [P, GE])
        psC = ps("psC", [P, GE])
        psD = ps("psD", [P, GE])
        psE = ps("psE", [P, GE])
        psS = ps("psS", [P, GE])

        s_const = sem("constants_made")
        s_w = sem("weights_loaded")
        s_pad = sem("index_pads_set")
        s_raw = sem("raw_indices_loaded")
        s_rawf = sem("raw_indices_float")
        s_dstrow = sem("dst_rows_stored")
        s_idxT = sem("indices_transposed")
        s_idx = sem("indices_ready")
        s_wueT = sem("wue_transposed")
        s_wueTs = sem("wue_copied")
        s_fold = sem("fold_multiplied")
        s_we = sem("edge_weights_ready")
        s_xl = [sem(f"x_loaded{i}") for i in range(2)]
        s_lastz = sem("last_block_cleared")
        s_two = sem("nodes_doubled")
        s_init = sem("sums_initialised")
        s_back = sem("sums_back")
        s_gath = [sem(f"rows_gathered{b}") for b in range(NB)]
        s_eh = [sem(f"edges_loaded{b}") for b in range(NB)]
        s_dstb = [sem(f"dst_broadcast{b}") for b in range(NB)]
        s_idxn = sem("idx_now_ready")
        s_T = sem("transposes_done")
        s_H = sem("hd_transposed")
        s_hsT = sem("hsT_ready")
        s_ehT = sem("ehT_ready")
        s_prod = sem("product_ready")
        s_A = sem("node1_done")
        s_B = sem("node2_done")
        s_C = sem("edge1_done")
        s_D = sem("edge2_done")
        s_E = sem("comb_done")
        s_S = sem("tile_sums_done")
        s_r1 = sem("relu_node_ready")
        s_r2 = sem("relu_edge_ready")
        s_m1 = sem("m1_copied")
        s_m12 = sem("m12_ready")
        s_msg = sem("messages_ready")
        s_same = sem("same_ready")
        s_tot = sem("totals_ready")
        s_put = sem("put_at_ready")
        s_v = sem("vector_chain")
        s_sc = [sem(f"scattered{b}") for b in range(2)]
        s_scq = sem("scatter_tile")
        s_ln = sem("norm_chain")
        s_cent = sem("centred")
        s_sq = sem("squared")
        s_ssq = sem("squares_summed")
        s_std = sem("std_ready")
        s_norm = sem("normalised")
        s_out = sem("stored")

        block = ctx.enter_context(nc.Block())

        def x_chunk(c):
            return x[c * LN_BLOCKS * P:(c + 1) * LN_BLOCKS * P, :].rearrange("(b p) d -> p b d", p=P)

        def node_chunk(c):
            return nodes[:, c * LW:(c + 1) * LW].rearrange("p (b d) -> p b d", d=D)

        N_FULL = (LN_BLOCKS - 1) * P
        LAST = (LC - 1) * LN_BLOCKS * P

        def move_last(eng, dram, to_dram, s):
            a = dram[LAST:LAST + N_FULL, :].rearrange("(b p) d -> p b d", p=P)
            sa = nodes[:, (LC - 1) * LW:(LC - 1) * LW + (LN_BLOCKS - 1) * D].rearrange("p (b d) -> p b d", d=D)
            t = dram[LAST + N_FULL:N, :]
            st = nodes[0:TAIL_N, (B - 1) * D:B * D]
            for u, v in ((a, sa), (t, st)):
                if to_dram:
                    eng.dma_start(u, v).then_inc(s, 16)
                else:
                    eng.dma_start(v, u).then_inc(s, 16)

        @block.sync
        def _(sp):
            sp.wait_ge(s_pad, 1)
            for k, a in enumerate((src, dst)):
                sp.dma_start(raw[:, k, 0:CH - 1, :], a[0:(CH - 1) * P * P].rearrange("(c t p) -> t c p", t=P, p=P)).then_inc(s_raw, 16)
                n_rows = FULL_T - (CH - 1) * P
                sp.dma_start(raw[0:n_rows, k, CH - 1, :], a[(CH - 1) * P * P:FULL_T * P].rearrange("(t p) -> t p", p=P)).then_inc(s_raw, 16)
                sp.dma_start(raw[n_rows:n_rows + 1, k, CH - 1, 0:TAIL_E], a[FULL_T * P:E].rearrange("(t p) -> t p", t=1)).then_inc(s_raw, 16)
            for t, a in ((w1, w_n1), (w2, w_n2), (we[D:P, :], w_e1), (we1_low, w_e1), (we2, w_e2), (wc, w_comb), (wue, w_ue),
                         (b1, b_n1.rearrange("(h a) -> h a", a=1)), (be1, b_e1.rearrange("(h a) -> h a", a=1))):
                sp.dma_start(t[:, :] if t is not we else t, a).then_inc(s_w, 16)
            sp.wait_ge(s_rawf, 1)
            sp.dma_start(dst_rows[0:(CH - 1) * P, :].rearrange("(c t) p -> t c p", t=P), rawf[:, 1, 0:CH - 1, :]).then_inc(s_dstrow, 16)
            sp.dma_start(dst_rows[(CH - 1) * P:T, :], rawf[0:TAIL_T, 1, CH - 1, :]).then_inc(s_dstrow, 16)
            sp.wait_ge(s_dstrow, 32)

            def load(g, b, prior, tail=0):
                if prior is not None:
                    sp.wait_ge(s_T, prior)
                    sp.wait_ge(s_put, prior)
                if tail:
                    sp.dma_start(xin[:, b, 0:tail - 1, D:2 * D], eh[g * GE:g * GE + (tail - 1) * P, :].rearrange("(j p) d -> p j d", p=P)).then_inc(s_eh[b], 16)
                    sp.dma_start(xin[0:TAIL_E, b, tail - 1, D:2 * D], eh[g * GE + (tail - 1) * P:E, :]).then_inc(s_eh[b], 16)
                else:
                    sp.dma_start(xin[:, b, :, D:2 * D], eh[bass.ds(g * GE, GE), :].rearrange("(j p) d -> p j d", p=P)).then_inc(s_eh[b], 16)
                rows = dst_rows.rearrange("(g j) p -> g (j p)", j=TPG)
                sp.dma_start(dst_all[:, b, :], rows[bass.ds(g, 1), :].partition_broadcast(P)[:, 0, :] if False else rows[bass.ds(g, 1), :].to_broadcast([P, GE])).then_inc(s_dstb[b], 16)

            for b in range(NB):
                load(b, b, None)
            for c in range(LC - 1):
                if c >= 2:
                    sp.wait_ge(s_two, c - 1)
                sp.dma_start(node_chunk(c), x_chunk(c)).then_inc(s_xl[c % 2], 16)
            sp.wait_ge(s_lastz, 1)
            sp.wait_ge(s_two, LC - 2)
            move_last(sp, x, False, s_xl[(LC - 1) % 2])
            for c in range(LC - 1):
                sp.wait_ge(s_two, c + 1)
                sp.dma_start(sums[c * LN_BLOCKS * P:(c + 1) * LN_BLOCKS * P, :].rearrange("(b p) d -> p b d", p=P), node_chunk(c)).then_inc(s_init, 16)
            sp.wait_ge(s_two, LC)
            move_last(sp, sums, True, s_init)

            with sp.Fori(NB, G - NB, NB) as g0:
                for b in range(NB):
                    load(g0 + b, b, g0 + (b - NB + 1))
            for b in range(NB):
                g = G - NB + b
                load(g, b, g - NB + 1, 0 if b < NB - 1 else FULL_T - (G - 1) * TPG + 1)
            sp.wait_ge(s_sc[0], 16 * TPG * (G // 2))
            sp.wait_ge(s_sc[1], 16 * TPG * (G // 2))
            for c in range(LC - 1):
                sp.dma_start(node_chunk(c), sums[c * LN_BLOCKS * P:(c + 1) * LN_BLOCKS * P, :].rearrange("(b p) d -> p b d", p=P)).then_inc(s_back, 16)
            move_last(sp, sums, False, s_back)
            for c in range(LC - 1):
                sp.wait_ge(s_norm, c + 1)
                sp.dma_start(out[c * LN_BLOCKS * P:(c + 1) * LN_BLOCKS * P, :].rearrange("(b p) d -> p b d", p=P), node_chunk(c)).then_inc(s_out, 16)
            sp.wait_ge(s_norm, LC)
            move_last(sp, out, True, s_out)
            sp.wait_ge(s_out, 16 * (LC + 1))

        @block.gpsimd
        def _(pool):
            nc.gpsimd.memset(ident[:], 0.0).then_inc(s_const, 1)
            nc.gpsimd.memset(lower[:], 1.0).then_inc(s_const, 1)
            nc.gpsimd.memset(eps[:], 1e-5).then_inc(s_const, 1)
            nc.gpsimd.iota(spare[:], pattern=[[0, T]], base=N, channel_multiplier=1, allow_small_or_imprecise_dtypes=True).then_inc(s_const, 1)
            pool.wait_ge(s_const, 4)
            nc.gpsimd.affine_select(out=ident[:], in_=ident[:], compare_op=ALU.not_equal, fill=1.0, base=0,
                                    pattern=[[-1, P]], channel_multiplier=1).then_inc(s_const, 1)
            nc.gpsimd.affine_select(out=lower[:], in_=lower[:], compare_op=ALU.is_gt, fill=0.0, base=0,
                                    pattern=[[-1, P]], channel_multiplier=1).then_inc(s_const, 1)

            counts = [pool.alloc_register(f"count{i}") for i in range(2 + TPG)]

            def held(i, value):
                if isinstance(value, int):
                    return value
                pool.reg_mov(counts[i], value)
                return counts[i]

            def settled():
                pool.wait_ge(s_const, 6)

            def gather(g, b, prior):
                turn = held(0, g + 1)
                prior = None if prior is None else held(1, prior)
                settled()
                pool.wait_ge(s_idxn, turn)
                if prior is not None:
                    pool.wait_ge(s_H, prior)
                for j in range(TPG):
                    nc.gpsimd.indirect_dma_start(out=xin[:, b, j, 0:D], out_offset=None, in_=x[:, :],
                                                 in_offset=bass.IndirectOffsetOnAxis(ap=idx_now[:, b, j:j + 1], axis=0)).then_inc(s_gath[b], 16)
                    nc.gpsimd.indirect_dma_start(out=hd[:, b, j, :], out_offset=None, in_=x[:, :],
                                                 in_offset=bass.IndirectOffsetOnAxis(ap=idx_now[:, b, TPG + j:TPG + j + 1], axis=0)).then_inc(s_gath[b], 16)

            def scatter(g, b, first):
                turn = held(0, g + 1)
                landed = [None if first and j == 0 else held(2 + j, g * (16 * TPG) + 16 * j) for j in range(TPG)]
                for j in range(TPG):
                    settled()
                    if j == 0:
                        pool.wait_ge(s_tot, turn)
                        pool.wait_ge(s_put, turn)
                    if landed[j] is not None:
                        pool.wait_ge(s_scq, landed[j])
                    nc.gpsimd.indirect_dma_start(out=sums[:, :], out_offset=bass.IndirectOffsetOnAxis(ap=put_at[:, b, j:j + 1], axis=0),
                                                 in_=tot[:, b, j, :], in_offset=None, compute_op=ALU.add).then_inc(s_scq, 16)

            for b in range(NB):
                gather(b, b, None)
            pool.wait_ge(s_init, 16 * (LC + 1))
            for b in range(NB):
                scatter(b, b, b == 0)
                gather(b + NB, b, b + 1)
            with pool.Fori(NB, G - NB, NB) as g0:
                for b in range(NB):
                    scatter(g0 + b, b, False)
                    gather(g0 + (b + NB), b, g0 + (b + 1))
            for b in range(NB):
                scatter(G - NB + b, b, False)
            pool.wait_ge(s_scq, 16 * T)
            pool.sem_inc(s_sc[0], 16 * TPG * (G // 2))
            pool.sem_inc(s_sc[1], 16 * TPG * (G // 2))

        @block.tensor
        def _(pe):
            pe.wait_ge(s_const, 6)
            pe.wait_ge(s_w, 16 * 9)
            nc.tensor.transpose(psA[0:D, 0:D], wue[:, :], ident[0:D, 0:D]).then_inc(s_wueT, 1)
            pe.wait_ge(s_wueTs, 1)
            nc.tensor.matmul(psB[0:D, 0:H], wueT[:, :], we1_low[:, :], start=True, stop=True).then_inc(s_fold, 1)
            pe.wait_ge(s_rawf, 1)
            for k, bank in ((0, psC), (1, psD)):
                for c in range(CH):
                    n = P if c < CH - 1 else TAIL_T
                    mm = nc.tensor.transpose(bank[:, c * P:c * P + n], rawf[0:n, k, c, :], ident[0:n, 0:n])
            mm.then_inc(s_idxT, 1)
            pe.wait_ge(s_we, 2)
            pe.wait_ge(s_idx, 3)

            def turn(g, b):
                n = g // NB + 1 if isinstance(g, int) else None
                return n

            def transposes(g, b, round_, prior, tail=False):
                pe.wait_ge(s_eh[b], 16 * round_ + (16 if tail else 0))
                pe.wait_ge(s_gath[b], 16 * 2 * TPG * round_)
                for j in range(TPG):
                    mm = nc.tensor.transpose(psT[:, j * P:(j + 1) * P], xin[:, b, j, :], ident[:, :])
                mm.then_inc(s_T, 1)
                for j in range(TPG):
                    mm = nc.tensor.transpose(psH[0:D, j * P:(j + 1) * P], hd[:, b, j, :], ident[:, :])
                mm.then_inc(s_H, 1)

            def comb(g):
                pe.wait_ge(s_m12, g + 1)
                for j in range(TPG):
                    mm = nc.tensor.matmul(psE[:, j * D:(j + 1) * D], m12[:, j * P:(j + 1) * P], wc[:, :], start=True, stop=True)
                mm.then_inc(s_E, 1)

            def tile_sums(g, b, first=False):
                pe.wait_ge(s_same, g + 1)
                pe.wait_ge(s_msg, g + 1)
                if not first:
                    pe.wait_ge(s_tot, g)
                for j in range(TPG):
                    mm = nc.tensor.matmul(psS[:, j * D:(j + 1) * D], same[:, b, j, :], msg[:, j, :], start=True, stop=True)
                mm.then_inc(s_S, 1)

            def step(g, b, nxt_round, first=False, last=False, tail=False):
                pe.wait_ge(s_hsT, g + 1)
                nc.tensor.matmul(psA[:, :], w1[:, :], hsT[:, :], start=True, stop=True).then_inc(s_A, 1)
                if not first:
                    comb(g - 1)
                pe.wait_ge(s_ehT, g + 1)
                pe.wait_ge(s_prod, g + 1)
                nc.tensor.matmul(psC[:, :], we[:, :], peT[:, :], start=True, stop=True).then_inc(s_C, 1)
                if not first:
                    tile_sums(g - 1, (b + 1) % NB, first="g1" if False else False) if not (isinstance(g, int) and g == 1) else tile_sums(0, 0, True)
                if not last:
                    transposes(g + 1, (b + 1) % NB, nxt_round, None, tail)
                pe.wait_ge(s_r1, g + 1)
                nc.tensor.matmul(psB[:, :], w2[:, :], r1[:, :], start=True, stop=True).then_inc(s_B, 1)
                pe.wait_ge(s_r2, g + 1)
                nc.tensor.matmul(psD[:, :], we2[:, :], r2[:, :], start=True, stop=True).then_inc(s_D, 1)

            transposes(0, 0, 1, None)
            step(0, 0, 1, first=True)
            step(1, 1, 2)
            with pe.Fori(1, G // NB - 1) as k:
                step(k * NB, 0, k + 1)
                step(k * NB + 1, 1, k + 2)
            step(G - 2, 0, G // NB, tail=True)
            step(G - 1, 1, None, last=True)
            comb(G - 1)
            tile_sums(G - 1, 1)

        @block.scalar
        def _(act):
            act.wait_ge(s_wueT, 1)
            nc.scalar.activation(wueT[:, :], psA[0:D, 0:D], ACT.Copy).then_inc(s_wueTs, 1)
            act.wait_ge(s_fold, 1)
            nc.scalar.activation(we[0:D, :], psB[0:D, 0:H], ACT.Copy, scale=0.2).then_inc(s_we, 1)
            act.wait_ge(s_w, 16 * 9)
            nc.scalar.activation(we[D:P, :], we[D:P, :], ACT.Copy, scale=0.8).then_inc(s_we, 1)

            def evacuate(g):
                act.wait_ge(s_T, g + 1)
                nc.scalar.activation(hsT[:, :], psT[0:D, :], ACT.Copy).then_inc(s_hsT, 1)
                nc.scalar.activation(peT[D:P, :], psT[D:P, :], ACT.Copy).then_inc(s_ehT, 1)

            def tanh(g):
                act.wait_ge(s_E, g + 1)
                nc.scalar.activation(msg[:, :, :].rearrange("p j d -> p (j d)"), psE[:, 0:TPG * D], ACT.Tanh).then_inc(s_msg, 1)

            def step(g, first=False, last=False):
                act.wait_ge(s_A, g + 1)
                nc.scalar.activation(r1[:, :], psA[:, :], ACT.Relu, bias=b1[:, 0:1]).then_inc(s_r1, 1)
                if not first:
                    tanh(g - 1)
                act.wait_ge(s_C, g + 1)
                nc.scalar.activation(r2[:, :], psC[:, :], ACT.Relu, bias=be1[:, 0:1]).then_inc(s_r2, 1)
                if not last:
                    evacuate(g + 1)
                act.wait_ge(s_B, g + 1)
                nc.scalar.activation(m1[:, :], psB[:, :], ACT.Copy).then_inc(s_m1, 1)

            for c in range(LC):
                act.wait_ge(s_xl[c % 2], 16 * (c // 2 + 1) + (16 if c == LC - 1 else 0))
                nc.scalar.activation(nodes[:, c * LW:(c + 1) * LW], nodes[:, c * LW:(c + 1) * LW], ACT.Copy, scale=2.0).then_inc(s_two, 1)
            evacuate(0)
            step(0, first=True)
            with act.Fori(1, G - 1) as g:
                step(g)
            step(G - 1, last=True)
            tanh(G - 1)
            for c in range(LC + 1):
                if c < LC:
                    act.wait_ge(s_cent, c + 1)
                    if c >= 2:
                        act.wait_ge(s_ssq, c - 1)
                    nc.scalar.activation(sq[:, c % 2, :], nodes[:, c * LW:(c + 1) * LW], ACT.Square).then_inc(s_sq, 1)
                if c >= 1:
                    act.wait_ge(s_ssq, c)
                    nc.scalar.activation(std[:, (c - 1) % 2, :], ssq[:, (c - 1) % 2, :], ACT.Sqrt, bias=eps[:, 0:1], scale=1.0 / D).then_inc(s_std, 1)

        @block.vector
        def _(dve):
            chain = [0]

            def link(ins):
                chain[0] += 1
                ins.then_inc(s_v, 1)
                dve.wait_ge(s_v, chain[0])

            nc.vector.memset(nodes[:, (B - 1) * D:B * D], 0.0).then_inc(s_lastz, 1)
            link(nc.vector.memset(raw[:, 0, CH - 1, :], 0))
            nc.vector.memset(raw[:, 1, CH - 1, :], N).then_inc(s_pad, 1)
            dve.wait_ge(s_raw, 16 * 6)
            dve.wait_ge(s_pad, 1)
            nc.vector.tensor_copy(rawf[:, :, :, :].rearrange("p k c t -> p (k c t)"), raw[:, :, :, :].rearrange("p k c t -> p (k c t)")).then_inc(s_rawf, 1)
            dve.wait_ge(s_idxT, 1)
            idx4 = idx[:, :, :]
            nc.vector.tensor_copy(idx4[:, :, 0:TPG], psC[:, 0:T].rearrange("p (g j) -> p g j", j=TPG)).then_inc(s_idx, 1)
            nc.vector.tensor_scalar(idx4[:, :, TPG:2 * TPG], psD[:, 0:T].rearrange("p (g j) -> p g j", j=TPG), float(N - 1), None, ALU.min).then_inc(s_idx, 1)
            nc.vector.tensor_copy(dstf[:, :], psD[:, 0:T]).then_inc(s_idx, 1)
            dve.wait_ge(s_idx, 3)
            dve.wait_ge(s_const, 6)
            link(nc.vector.tensor_tensor(spare[:, :], spare[:, :], dstf[:, :], ALU.subtract))

            def indices(g, b, prior):
                if prior is not None:
                    dve.wait_ge(s_gath[b], prior)
                nc.vector.tensor_copy(idx_now[:, b, :].rearrange("p (a j) -> p a j", a=1), idx[:, bass.ds(g, 1), :]).then_inc(s_idxn, 1)

            def product(g):
                dve.wait_ge(s_H, g + 1)
                dve.wait_ge(s_hsT, g + 1)
                nc.vector.tensor_tensor(peT[0:D, :], psH[0:D, :], hsT[:, :], ALU.mult).then_inc(s_prod, 1)

            VC = 3
            V0 = chain[0]

            def equal_dst(g, b, round_, prior):
                dve.wait_ge(s_dstb[b], 16 * round_)
                for j in range(TPG):
                    i = nc.vector.tensor_scalar(same[:, b, j, :], dst_all[:, b, j * P:(j + 1) * P],
                                            dstf[:, bass.ds(g * TPG + j, 1)], None, ALU.is_equal)
                i.then_inc(s_same, 1)
                dve.wait_ge(s_same, g + 1)
                for j in range(TPG):
                    i = nc.vector.tensor_tensor_reduce(junk[:, j, :], same[:, b, j, :], lower[:, :], 1.0, 0.0, ALU.mult, ALU.add, earlier[:, j:j + 1])
                i.then_inc(s_v, 1)
                dve.wait_ge(s_v, g * VC + (V0 + 1))
                nc.vector.tensor_scalar(dup[:, :], earlier[:, :], 1.0, None, ALU.min).then_inc(s_v, 1)
                dve.wait_ge(s_v, g * VC + (V0 + 2))
                nc.vector.tensor_tensor(moved[:, :], dup[:, :], spare[:, bass.ds(g * TPG, TPG)], ALU.mult).then_inc(s_v, 1)
                dve.wait_ge(s_v, g * VC + (V0 + 3))
                if prior is not None:
                    dve.wait_ge(s_scq, prior * (16 * TPG))
                nc.vector.tensor_tensor(put_at[:, b, :], moved[:, :], dstf[:, bass.ds(g * TPG, TPG)], ALU.add).then_inc(s_put, 1)

            def totals(g, b, prior):
                dve.wait_ge(s_S, g + 1)
                if prior is not None:
                    dve.wait_ge(s_scq, prior * (16 * TPG))
                nc.vector.tensor_copy(tot[:, b, :, :].rearrange("p j d -> p (j d)"), psS[:, 0:TPG * D]).then_inc(s_tot, 1)

            def step(g, b, round_, first=False, last=False, peeled=False):
                pr = None if peeled else g - (NB - 1)
                if not last:
                    indices(g + NB, b, round_ * (16 * 2 * TPG)) if not last else None
                equal_dst(g, b, round_, pr)
                if not first:
                    totals(g - 1, (b + 1) % NB, None if (peeled) else g - NB)
                product(g + 1)
                dve.wait_ge(s_D, g + 1)
                dve.wait_ge(s_m1, g + 1)
                nc.vector.tensor_tensor(m12[:, :], psD[:, :], m1[:, :], ALU.mult).then_inc(s_m12, 1)

            def step_end(g, b, round_, more):
                equal_dst(g, b, round_, g - (NB - 1))
                totals(g - 1, (b + 1) % NB, g - NB)
                if more:
                    product(g + 1)
                dve.wait_ge(s_D, g + 1)
                dve.wait_ge(s_m1, g + 1)
                nc.vector.tensor_tensor(m12[:, :], psD[:, :], m1[:, :], ALU.mult).then_inc(s_m12, 1)

            for b in range(NB):
                indices(b, b, None)
            product(0)
            step(0, 0, 1, first=True, peeled=True)
            step(1, 1, 1, peeled=True)
            with dve.Fori(1, G // NB - 1) as k:
                step(k * NB, 0, k + 1)
                step(k * NB + 1, 1, k + 1)
            step_end(G - 2, 0, G // NB, True)
            step_end(G - 1, 1, G // NB, False)
            totals(G - 1, 1, G - NB)

            dve.wait_ge(s_back, 16 * (LC + 1))
            def scale_out(c):
                dve.wait_ge(s_std, c + 1)
                nc.vector.reciprocal(rstd[:, c % 2, :], std[:, c % 2, :]).then_inc(s_ln, 1)
                ln[0] += 1
                dve.wait_ge(s_ln, ln[0])
                nc.vector.tensor_tensor(node_chunk(c), node_chunk(c), rstd[:, c % 2, :].rearrange("p (b a) -> p b a", a=1).to_broadcast([P, LN_BLOCKS, D]), ALU.mult).then_inc(s_norm, 1)

            ln = [0]
            for c in range(LC + 1):
                if c < LC:
                    nc.vector.tensor_reduce(mean[:, c % 2, :], node_chunk(c), AX_X, ALU.add).then_inc(s_ln, 1)
                    ln[0] += 1
                    dve.wait_ge(s_ln, ln[0])
                    nc.vector.tensor_scalar(nmean[:, c % 2, :], mean[:, c % 2, :], 1.0 / D, None, ALU.mult).then_inc(s_ln, 1)
                    ln[0] += 1
                    dve.wait_ge(s_ln, ln[0])
                    nc.vector.tensor_tensor(node_chunk(c), node_chunk(c), nmean[:, c % 2, :].rearrange("p (b a) -> p b a", a=1).to_broadcast([P, LN_BLOCKS, D]), ALU.subtract).then_inc(s_cent, 1)
                if c >= 1:
                    scale_out(c - 1)
                if c < LC:
                    dve.wait_ge(s_sq, c + 1)
                    if c >= 2:
                        dve.wait_ge(s_std, c - 1)
                    nc.vector.tensor_reduce(ssq[:, c % 2, :], sq[:, c % 2, :].rearrange("p (b d) -> p b d", d=D), AX_X, ALU.add).then_inc(s_ssq, 1)


_INS = ['x', 'src', 'dst', 'edge_attr_64', 'L0_gnn_W_node1', 'L0_gnn_b_node1', 'L0_gnn_W_node2', 'L0_gnn_W_edge1',
        'L0_gnn_b_edge1', 'L0_gnn_W_edge2', 'L0_gnn_W_comb', 'L0_gnn_W_ue']


def kernel(**inputs):
    import numpy as _np
    import concourse.bacc as _bacc
    from concourse import mybir as _mybir
    from concourse.bass_utils import run_bass_kernel_spmd as _run

    nc = _bacc.Bacc("TRN2", target_bir_lowering=False, num_devices=1)
    arrays, args = {}, []
    for name in _INS:
        a = _np.ascontiguousarray(inputs[name])
        arrays[f"in_{name}_dram"] = a
        args.append(nc.dram_tensor(f"in_{name}_dram", a.shape, _mybir.dt.from_np(a.dtype), kind="ExternalInput").ap())
    args.append(nc.dram_tensor("out_dram", (50000, 64), _mybir.dt.float32, kind="ExternalOutput").ap())
    gnn_kernel(nc, *args)
    r = _run(nc, [arrays], core_ids=[0])
    return r.results[0]["out_dram"]
```

```python
from contextlib import ExitStack

import concourse.bass as bass
from concourse import mybir

P = 128
F32 = mybir.dt.float32
I32 = mybir.dt.int32
F16 = mybir.dt.float16
BF16 = mybir.dt.bfloat16
ALU = mybir.AluOpType
ACT = mybir.ActivationFunctionType
AX_X = mybir.AxisListType.X

TPG = 4
NB = 2
LN_BLOCKS = 23

WK = 2
WP = 96
WIN = WK * WP
OHB = 3
SPAN = 4
GB = SPAN + OHB
NEAR = 8
PRE = 8
SCALE = 4096.0


def gnn_kernel(nc, x, src, dst, eh, w_n1, b_n1, w_n2, w_e1, b_e1, w_e2, w_comb, w_ue, out):
    N, D = x.shape
    E = src.shape[0]
    H = w_n1.shape[1]
    G = -(-E // (P * TPG))
    T = G * TPG
    GE = P * TPG
    FULL_T = E // P
    TAIL_E = E - FULL_T * P
    CH = -(-T // P)
    TAIL_T = T - (CH - 1) * P
    B = -(-N // P)
    TAIL_N = N - (B - 1) * P
    LC = B // LN_BLOCKS
    assert LC * LN_BLOCKS == B and G % NB == 0 and D == 64 and H == P
    LW = LN_BLOCKS * D
    CB = TPG
    CW = CB * D
    TAIL_B = B - (G - 1) * CB
    assert -(-B // CB) == G and 0 < TAIL_B <= CB
    PAD_B = G * CB + GB + 1

    with ExitStack() as ctx:
        def sb(name, shape, dt=F32):
            return ctx.enter_context(nc.sbuf_tensor(name, shape, dt))

        def ps(name, shape, dt=F32):
            return ctx.enter_context(nc.psum_tensor(name, shape, dt))

        def sem(name):
            return ctx.enter_context(nc.semaphore(name))

        dst_rows = nc.dram_tensor("dst_rows", (T, P), F32, kind="Internal").ap()
        dst_local = nc.dram_tensor("dst_local", (T, P), F16, kind="Internal").ap()
        x_parts = nc.dram_tensor("x_parts", (G * GE, 3 * D), BF16, kind="Internal").ap()
        sums = nc.dram_tensor("node_sums", (N + P, D), F32, kind="Internal").ap()

        ident = sb("ident", [P, P])
        lower = sb("lower", [P, P])
        w1 = sb("w1", [D, H])
        w2 = sb("w2", [H, H])
        we = sb("we", [P, H])
        we1_low = sb("we1_low", [D, H])
        we2 = sb("we2", [H, H])
        wc = sb("wc", [H, D])
        wue = sb("wue", [D, D])
        wueT = sb("wueT", [D, D])
        b1 = sb("b1", [H, 1])
        be1 = sb("be1", [H, 1])
        eps = sb("eps", [P, 1])
        raw = sb("raw", [P, 2, CH, P], I32)
        rawf = sb("rawf", [P, 2, CH, P])
        idx = sb("idx", [P, G, 2 * TPG], I32)
        dstf = sb("dstf", [P, T])
        spare = sb("spare", [P, T])
        idx_now = sb("idx_now", [P, NB, 2 * TPG], I32)
        nodes = sb("nodes", [P, PAD_B * D])
        xin = sb("xin", [P, NB, TPG, 2 * D])
        hd = sb("hd", [P, NB, TPG, D])
        dst_all = sb("dst_all", [P, NB, GE])
        hsT = sb("hsT", [D, GE])
        peT = sb("peT", [P, GE])
        r1 = sb("r1", [H, GE])
        r2 = sb("r2", [H, GE])
        m1 = sb("m1", [H, GE])
        m12 = sb("m12", [H, GE])
        msg = sb("msg", [P, TPG, D])
        same = sb("same", [P, 2, TPG, P])
        junk = sb("junk", [P, TPG, P])
        earlier = sb("earlier", [P, TPG])
        dup = sb("dup", [P, TPG])
        moved = sb("moved", [P, TPG])
        put_at = sb("put_at", [P, 2, TPG], I32)
        tot = sb("tot", [P, 2, TPG, D])
        sq = sb("sq", [P, 2, LW])
        mean = sb("mean", [P, 2, LN_BLOCKS])
        nmean = sb("nmean", [P, 2, LN_BLOCKS])
        ssq = sb("ssq", [P, 2, LN_BLOCKS])
        std = sb("std", [P, 2, LN_BLOCKS])
        rstd = sb("rstd", [P, 2, LN_BLOCKS])

        row_min = sb("row_min", [P, CH])
        row_max = sb("row_max", [P, CH])
        row_base = sb("row_base", [P, CH])
        row_span = sb("row_span", [P, CH])
        row_mini = sb("row_mini", [P, CH], I32)
        row_alii = sb("row_alii", [P, CH], I32)
        row_ali = sb("row_ali", [P, CH])
        row_loc = sb("row_loc", [P, CH, P], F16)
        ones = sb("ones", [1, P])
        g_start = sb("g_start", [1, G])
        t_ali = sb("t_ali", [1, T])
        t_off = sb("t_off", [1, T])
        g_ali = sb("g_ali", [1, G])
        g_dev = sb("g_dev", [1, G])
        worst = sb("worst", [1, 4])
        excess = sb("excess", [1, 4])
        most = sb("most", [1, 1])
        near = sb("near", [1, 1], I32)
        t_base_i = sb("t_base_i", [1, T], I32)
        t_off_i = sb("t_off_i", [1, T], I32)
        g_col_i = sb("g_col_i", [1, G], I32)
        w1_even = sb("w1_even", [P, H])
        w1_odd = sb("w1_odd", [P, H])
        wc_wide = sb("wc_wide", [H, P])
        win_at = sb("win_at", [WP, WK])
        block_at = sb("block_at", [P, OHB * P], F16)
        zeros = sb("zeros", [P, GB * D], F16)
        half_neg = sb("half_neg", [P, CB])
        dst_in_block = sb("dst_in_block", [P, T])
        hs = hd
        pe_in = xin
        src_now = sb("src_now", [P, NB, TPG], I32)
        x_win = sb("x_win", [WP, NB, TPG, WK, 3 * D], BF16)
        dst_win = sb("dst_win", [WP, NB, GE], F16)
        pick = sb("pick", [WP, NB, WK, GE], BF16)
        put = sb("put", [P, NB, TPG, OHB * P], F16)
        hsP = sb("hsP", [P, 2 * P])
        comb_sb = sb("comb_sb", [P, GE])
        msg_hi = sb("msg_hi", [P, TPG, D], F16)
        msg_lo = sb("msg_lo", [P, TPG, D], F16)
        x_in = sb("x_in", [P, 2, CB, D])
        x_rest = sb("x_rest", [P, 2, CB, D])
        x_split = sb("x_split", [P, 2, CB, 3 * D], BF16)
        stats = sb("stats", [P, 2, CB, 6])
        mv = sb("mv", [P, 2, CB, 2])
        var_eps = sb("var_eps", [P, 2, CB])
        inv_std = sb("inv_std", [P, 2, CB])

        psT = ps("psT", [P, GE])
        psH = ps("psH", [P, GE])
        psA = ps("psA", [P, GE])
        psB = ps("psB", [P, GE])
        psC = ps("psC", [P, GE])
        psD = ps("psD", [P, GE])
        psE = ps("psE", [P, GE])
        psS = ps("psS", [P, GE])

        s_const = sem("constants_made")
        s_w = sem("weights_loaded")
        s_pad = sem("index_pads_set")
        s_raw = sem("raw_indices_loaded")
        s_rawf = sem("raw_indices_float")
        s_dstrow = sem("dst_rows_stored")
        s_idxT = sem("indices_transposed")
        s_idx = sem("indices_ready")
        s_wueT = sem("wue_transposed")
        s_wueTs = sem("wue_copied")
        s_fold = sem("fold_multiplied")
        s_we = sem("edge_weights_ready")
        s_xl = [sem(f"x_loaded{i}") for i in range(2)]
        s_lastz = sem("last_block_cleared")
        s_two = sem("nodes_doubled")
        s_init = sem("sums_initialised")
        s_back = sem("sums_back")
        s_gath = [sem(f"rows_gathered{b}") for b in range(NB)]
        s_eh = [sem(f"edges_loaded{b}") for b in range(NB)]
        s_dstb = [sem(f"dst_broadcast{b}") for b in range(NB)]
        s_idxn = sem("idx_now_ready")
        s_T = sem("transposes_done")
        s_H = sem("hd_transposed")
        s_hsT = sem("hsT_ready")
        s_ehT = sem("ehT_ready")
        s_prod = sem("product_ready")
        s_A = sem("node1_done")
        s_B = sem("node2_done")
        s_C = sem("edge1_done")
        s_D = sem("edge2_done")
        s_E = sem("comb_done")
        s_S = sem("tile_sums_done")
        s_r1 = sem("relu_node_ready")
        s_r2 = sem("relu_edge_ready")
        s_m1 = sem("m1_copied")
        s_m12 = sem("m12_ready")
        s_msg = sem("messages_ready")
        s_same = sem("same_ready")
        s_tot = sem("totals_ready")
        s_put = sem("put_at_ready")
        s_v = sem("vector_chain")
        s_sc = [sem(f"scattered{b}") for b in range(2)]
        s_scq = sem("scatter_tile")
        s_ln = sem("norm_chain")
        s_cent = sem("centred")
        s_sq = sem("squared")
        s_ssq = sem("squares_summed")
        s_std = sem("std_ready")
        s_norm = sem("normalised")
        s_out = sem("stored")

        s_w1o = sem("w1_odd_loaded")
        s_row = sem("row_chain")
        s_rowv = sem("row_values_ready")
        s_local = sem("dst_local_stored")
        s_rowT = sem("row_values_transposed")
        s_ali = sem("aligned_row_ready")
        s_alib = sem("aligned_spread")
        s_guard = sem("guard_ready")
        s_near = sem("near_constants_ready")
        s_xin = [sem(f"x_chunk_loaded{b}") for b in range(2)]
        s_hi = sem("x_high_ready")
        s_rest = sem("x_rest_ready")
        s_mid = sem("x_middle_ready")
        s_low = sem("x_low_ready")
        s_xst = [sem(f"x_parts_stored{b}") for b in range(2)]
        s_win = [sem(f"windows_loaded{b}") for b in range(NB)]
        s_dwin = [sem(f"window_dst_loaded{b}") for b in range(NB)]
        s_srcn = sem("src_now_ready")
        s_pick = sem("pick_ready")
        s_hd = sem("hd_picked")
        s_putr = sem("put_ready")
        s_hsP = sem("hsP_ready")
        s_comb = sem("comb_copied")
        s_M = sem("comb_transposed")
        s_tanh = sem("tanh_ready")
        s_mhi = sem("message_high_ready")
        s_mlo = sem("message_low_ready")
        s_agg = sem("group_summed")
        s_add = sem("sums_added")
        s_stats = sem("stats_ready")
        s_mv = sem("mean_var_ready")
        s_eps = sem("eps_added")
        s_inv = sem("inverse_std_ready")

        block = ctx.enter_context(nc.Block())

        def x_chunk(c):
            return x[c * LN_BLOCKS * P:(c + 1) * LN_BLOCKS * P, :].rearrange("(b p) d -> p b d", p=P)

        def node_chunk(c):
            return nodes[:, c * LW:(c + 1) * LW].rearrange("p (b d) -> p b d", d=D)

        N_FULL = (LN_BLOCKS - 1) * P
        LAST = (LC - 1) * LN_BLOCKS * P

        def move_last(eng, dram, to_dram, s):
            a = dram[LAST:LAST + N_FULL, :].rearrange("(b p) d -> p b d", p=P)
            sa = nodes[:, (LC - 1) * LW:(LC - 1) * LW + (LN_BLOCKS - 1) * D].rearrange("p (b d) -> p b d", d=D)
            t = dram[LAST + N_FULL:N, :]
            st = nodes[0:TAIL_N, (B - 1) * D:B * D]
            for u, v in ((a, sa), (t, st)):
                if to_dram:
                    eng.dma_start(u, v).then_inc(s, 16)
                else:
                    eng.dma_start(v, u).then_inc(s, 16)

        PEEL = 12
        LOOP_END = (G - PRE - 2) // 2 * 2
        OUT_LAG = 7

        def in_range(i, lag):
            return not isinstance(i, int) or 0 <= i + lag < G

        @block.sync
        def _(sp):
            sp.wait_ge(s_pad, 1)
            for k, a in enumerate((src, dst)):
                sp.dma_start(raw[:, k, 0:CH - 1, :], a[0:(CH - 1) * P * P].rearrange("(c t p) -> t c p", t=P, p=P)).then_inc(s_raw, 16)
                n_rows = FULL_T - (CH - 1) * P
                sp.dma_start(raw[0:n_rows, k, CH - 1, :], a[(CH - 1) * P * P:FULL_T * P].rearrange("(t p) -> t p", p=P)).then_inc(s_raw, 16)
                sp.dma_start(raw[n_rows:n_rows + 1, k, CH - 1, 0:TAIL_E], a[FULL_T * P:E].rearrange("(t p) -> t p", t=1)).then_inc(s_raw, 16)
            for t, a in ((w1, w_n1), (w2, w_n2), (we[D:P, :], w_e1), (we1_low, w_e1), (we2, w_e2), (wc, w_comb), (wue, w_ue),
                         (b1, b_n1.rearrange("(h a) -> h a", a=1)), (be1, b_e1.rearrange("(h a) -> h a", a=1))):
                sp.dma_start(t[:, :] if t is not we else t, a).then_inc(s_w, 16)
            sp.wait_ge(s_rowv, 1)
            sp.dma_start(dst_local[0:(CH - 1) * P, :].rearrange("(c t) p -> t c p", t=P), row_loc[:, 0:CH - 1, :]).then_inc(s_local, 16)
            sp.dma_start(dst_local[(CH - 1) * P:T, :], row_loc[0:TAIL_T, CH - 1, :]).then_inc(s_local, 16)
            sp.dma_start(dst_rows[0:(CH - 1) * P, :].rearrange("(c t) p -> t c p", t=P), rawf[:, 1, 0:CH - 1, :]).then_inc(s_dstrow, 16)
            sp.dma_start(dst_rows[(CH - 1) * P:T, :], rawf[0:TAIL_T, 1, CH - 1, :]).then_inc(s_dstrow, 16)
            sp.wait_ge(s_dstrow, 32)

            sp.wait_ge(s_local, 32)
            sp.wait_ge(s_guard, 1)

            def load_x(c, b):
                if isinstance(c, int) and c == G - 1:
                    a = x[c * GE:c * GE + (TAIL_B - 1) * P, :].rearrange("(b p) d -> p b d", p=P)
                    sp.dma_start(x_in[:, b, 0:TAIL_B - 1, :], a).then_inc(s_xin[b], 16)
                    sp.dma_start(x_in[0:TAIL_N, b, TAIL_B - 1, :], x[(B - 1) * P:N, :]).then_inc(s_xin[b], 16)
                else:
                    sp.dma_start(x_in[:, b, :, :], x[bass.ds(c * GE, GE), :].rearrange("(b p) d -> p b d", p=P)).then_inc(s_xin[b], 16)

            def store_split(c, b):
                sp.wait_ge(s_low, c + 1)
                sp.dma_start(x_parts[bass.ds(c * GE, GE), :].rearrange("(b p) d -> p b d", p=P), x_split[:, b, :, :]).then_inc(s_xst[b], 16)

            def load_group(g, b, fresh, stored0, stored1):
                if not fresh:
                    sp.wait_ge(s_hd, g - (NB - 1))
                sp.wait_ge(s_xst[0], stored0)
                sp.wait_ge(s_xst[1], stored1)
                for j in range(TPG):
                    first = sp.value_load(t_base_i[0:1, bass.ds(g * TPG + j, 1)], min_val=0, max_val=N - WIN)
                    sp.dma_start(x_win[:, b, j, :, :], x_parts[bass.ds(first, WIN), :].rearrange("(p k) d -> p k d", k=WK)).then_inc(s_win[b], 16)
                if not fresh:
                    sp.wait_ge(s_pick, g - (NB - 1))
                sp.dma_start(dst_win[:, b, :], dst_local.rearrange("(g j) p -> g (j p)", j=TPG)[bass.ds(g, 1), :].to_broadcast([WP, GE])).then_inc(s_dwin[b], 16)
                if not fresh:
                    sp.wait_ge(s_T, g - (NB - 1))
                if isinstance(g, int) and g == G - 1:
                    tail = FULL_T - g * TPG + 1
                    sp.dma_start(pe_in[:, b, 0:tail - 1, D:2 * D], eh[g * GE:g * GE + (tail - 1) * P, :].rearrange("(j p) d -> p j d", p=P)).then_inc(s_eh[b], 16)
                    sp.dma_start(pe_in[0:TAIL_E, b, tail - 1, D:2 * D], eh[g * GE + (tail - 1) * P:E, :]).then_inc(s_eh[b], 16)
                else:
                    sp.dma_start(pe_in[:, b, :, D:2 * D], eh[bass.ds(g * GE, GE), :].rearrange("(j p) d -> p j d", p=P)).then_inc(s_eh[b], 16)

            def store_out(c):
                sp.wait_ge(s_norm, c + 1)
                if isinstance(c, int) and c == G - 1:
                    a = out[c * GE:c * GE + (TAIL_B - 1) * P, :].rearrange("(b p) d -> p b d", p=P)
                    sp.dma_start(a, nodes[:, c * CW:c * CW + (TAIL_B - 1) * D].rearrange("p (b d) -> p b d", d=D)).then_inc(s_out, 16)
                    sp.dma_start(out[(B - 1) * P:N, :], nodes[0:TAIL_N, (B - 1) * D:B * D]).then_inc(s_out, 16)
                else:
                    sp.dma_start(out[bass.ds(c * GE, GE), :].rearrange("(b p) d -> p b d", p=P),
                                 nodes[:, bass.ds(c * CW, CW)].rearrange("p (b d) -> p b d", d=D)).then_inc(s_out, 16)

            def near_step(i, b, half):
                if in_range(i, 2):
                    n = (half + 3) * 16 if not isinstance(i, int) else None
                    s0 = n if n is not None else 16 * ((min(i + 5, G - 1)) // 2 + 1)
                    s1 = n if n is not None else 16 * ((min(i + 5, G - 1) + 1) // 2)
                    load_group(i + 2, b, False, s0, s1)
                if in_range(i, PRE - 2):
                    store_split(i + (PRE - 2), b)
                if in_range(i, PRE + 1):
                    sp.wait_ge(s_rest, i + PRE)
                    sp.wait_ge(s_two, i + PRE)
                    load_x(i + (PRE + 1), (b + 1) % 2)
                if in_range(i, -OUT_LAG):
                    store_out(i - OUT_LAG)

            with sp.If(sp.value_load(near[0:1, 0:1], min_val=0, max_val=1)):
                load_x(0, 0)
                load_x(1, 1)
                for c in range(2, PRE + 1):
                    sp.wait_ge(s_rest, c - 1)
                    sp.wait_ge(s_two, c - 1)
                    load_x(c, c % 2)
                    store_split(c - 2, c % 2) if c - 2 < PRE - 2 else None
                for b in range(NB):
                    load_group(b, b, True, 16 * ((b + 3) // 2 + 1), 16 * ((b + 4) // 2))
                for i in range(PEEL):
                    near_step(i, i % 2, None)
                with sp.Fori(PEEL // 2, LOOP_END // 2) as k:
                    for b in range(2):
                        near_step(k * 2 + b, b, k)
                for i in range(LOOP_END, G + OUT_LAG):
                    near_step(i, i % 2, None)
                sp.wait_ge(s_out, 16 * (G + 1))
            with sp.Else():
                def load(g, b, prior, tail=0):
                    if prior is not None:
                        sp.wait_ge(s_T, prior)
                        sp.wait_ge(s_put, prior)
                    if tail:
                        sp.dma_start(xin[:, b, 0:tail - 1, D:2 * D], eh[g * GE:g * GE + (tail - 1) * P, :].rearrange("(j p) d -> p j d", p=P)).then_inc(s_eh[b], 16)
                        sp.dma_start(xin[0:TAIL_E, b, tail - 1, D:2 * D], eh[g * GE + (tail - 1) * P:E, :]).then_inc(s_eh[b], 16)
                    else:
                        sp.dma_start(xin[:, b, :, D:2 * D], eh[bass.ds(g * GE, GE), :].rearrange("(j p) d -> p j d", p=P)).then_inc(s_eh[b], 16)
                    rows = dst_rows.rearrange("(g j) p -> g (j p)", j=TPG)
                    sp.dma_start(dst_all[:, b, :], rows[bass.ds(g, 1), :].partition_broadcast(P)[:, 0, :] if False else rows[bass.ds(g, 1), :].to_broadcast([P, GE])).then_inc(s_dstb[b], 16)

                for b in range(NB):
                    load(b, b, None)
                for c in range(LC - 1):
                    if c >= 2:
                        sp.wait_ge(s_two, c - 1)
                    sp.dma_start(node_chunk(c), x_chunk(c)).then_inc(s_xl[c % 2], 16)
                sp.wait_ge(s_lastz, 1)
                sp.wait_ge(s_two, LC - 2)
                move_last(sp, x, False, s_xl[(LC - 1) % 2])
                for c in range(LC - 1):
                    sp.wait_ge(s_two, c + 1)
                    sp.dma_start(sums[c * LN_BLOCKS * P:(c + 1) * LN_BLOCKS * P, :].rearrange("(b p) d -> p b d", p=P), node_chunk(c)).then_inc(s_init, 16)
                sp.wait_ge(s_two, LC)
                move_last(sp, sums, True, s_init)

                with sp.Fori(NB, G - NB, NB) as g0:
                    for b in range(NB):
                        load(g0 + b, b, g0 + (b - NB + 1))
                for b in range(NB):
                    g = G - NB + b
                    load(g, b, g - NB + 1, 0 if b < NB - 1 else FULL_T - (G - 1) * TPG + 1)
                sp.wait_ge(s_sc[0], 16 * TPG * (G // 2))
                sp.wait_ge(s_sc[1], 16 * TPG * (G // 2))
                for c in range(LC - 1):
                    sp.dma_start(node_chunk(c), sums[c * LN_BLOCKS * P:(c + 1) * LN_BLOCKS * P, :].rearrange("(b p) d -> p b d", p=P)).then_inc(s_back, 16)
                move_last(sp, sums, False, s_back)
                for c in range(LC - 1):
                    sp.wait_ge(s_norm, c + 1)
                    sp.dma_start(out[c * LN_BLOCKS * P:(c + 1) * LN_BLOCKS * P, :].rearrange("(b p) d -> p b d", p=P), node_chunk(c)).then_inc(s_out, 16)
                sp.wait_ge(s_norm, LC)
                move_last(sp, out, True, s_out)
                sp.wait_ge(s_out, 16 * (LC + 1))

        @block.gpsimd
        def _(pool):
            nc.gpsimd.memset(ident[:], 0.0).then_inc(s_const, 1)
            nc.gpsimd.memset(lower[:], 1.0).then_inc(s_const, 1)
            nc.gpsimd.memset(eps[:], 1e-5).then_inc(s_const, 1)
            nc.gpsimd.iota(spare[:], pattern=[[0, T]], base=N, channel_multiplier=1, allow_small_or_imprecise_dtypes=True).then_inc(s_const, 1)
            nc.gpsimd.iota(g_start[:], pattern=[[GE, G]], base=0, channel_multiplier=0, allow_small_or_imprecise_dtypes=True).then_inc(s_const, 1)
            nc.gpsimd.memset(ones[:], 1.0).then_inc(s_const, 1)
            nc.gpsimd.iota(win_at[:], pattern=[[1, WK]], base=0, channel_multiplier=WK, allow_small_or_imprecise_dtypes=True).then_inc(s_near, 1)
            nc.gpsimd.iota(block_at[:], pattern=[[1, OHB * P]], base=0, channel_multiplier=0, allow_small_or_imprecise_dtypes=True).then_inc(s_near, 1)
            nc.gpsimd.memset(zeros[:], 0.0).then_inc(s_near, 1)
            nc.gpsimd.memset(half_neg[:], -0.5).then_inc(s_near, 1)
            nc.gpsimd.memset(nodes[:, G * CW:PAD_B * D], 0.0).then_inc(s_near, 1)
            nc.gpsimd.memset(x_in[:], 0.0).then_inc(s_near, 1)
            nc.gpsimd.memset(wc_wide[:, D:P], 0.0).then_inc(s_near, 1)
            pool.wait_ge(s_const, 6)
            nc.gpsimd.affine_select(out=ident[:], in_=ident[:], compare_op=ALU.not_equal, fill=1.0, base=0,
                                    pattern=[[-1, P]], channel_multiplier=1).then_inc(s_const, 1)
            nc.gpsimd.affine_select(out=lower[:], in_=lower[:], compare_op=ALU.is_gt, fill=0.0, base=0,
                                    pattern=[[-1, P]], channel_multiplier=1).then_inc(s_const, 1)

            counts = [pool.alloc_register(f"count{i}") for i in range(2 + TPG)]

            def held(i, value):
                if isinstance(value, int):
                    return value
                pool.reg_mov(counts[i], value)
                return counts[i]

            def settled():
                pool.wait_ge(s_const, 8)

            def gather(g, b, prior):
                turn = held(0, g + 1)
                prior = None if prior is None else held(1, prior)
                settled()
                pool.wait_ge(s_idxn, turn)
                if prior is not None:
                    pool.wait_ge(s_H, prior)
                for j in range(TPG):
                    nc.gpsimd.indirect_dma_start(out=xin[:, b, j, 0:D], out_offset=None, in_=x[:, :],
                                                 in_offset=bass.IndirectOffsetOnAxis(ap=idx_now[:, b, j:j + 1], axis=0)).then_inc(s_gath[b], 16)
                    nc.gpsimd.indirect_dma_start(out=hd[:, b, j, :], out_offset=None, in_=x[:, :],
                                                 in_offset=bass.IndirectOffsetOnAxis(ap=idx_now[:, b, TPG + j:TPG + j + 1], axis=0)).then_inc(s_gath[b], 16)

            def scatter(g, b, first):
                turn = held(0, g + 1)
                landed = [None if first and j == 0 else held(2 + j, g * (16 * TPG) + 16 * j) for j in range(TPG)]
                for j in range(TPG):
                    settled()
                    if j == 0:
                        pool.wait_ge(s_tot, turn)
                        pool.wait_ge(s_put, turn)
                    if landed[j] is not None:
                        pool.wait_ge(s_scq, landed[j])
                    nc.gpsimd.indirect_dma_start(out=sums[:, :], out_offset=bass.IndirectOffsetOnAxis(ap=put_at[:, b, j:j + 1], axis=0),
                                                 in_=tot[:, b, j, :], in_offset=None, compute_op=ALU.add).then_inc(s_scq, 16)

            def gather_src(g, b, fresh):
                turn = held(0, g + 1)
                prior = held(1, g - (NB - 1))
                settled()
                pool.wait_ge(s_srcn, turn)
                if not fresh:
                    pool.wait_ge(s_T, prior)
                for j in range(TPG):
                    nc.gpsimd.indirect_dma_start(out=hs[:, b, j, :], out_offset=None, in_=x[:, :],
                                                 in_offset=bass.IndirectOffsetOnAxis(ap=src_now[:, b, j:j + 1], axis=0)).then_inc(s_gath[b], 16)

            def inverse_std(c, b):
                pool.wait_ge(s_eps, c + 1)
                if not isinstance(c, int) or c >= 2:
                    pool.wait_ge(s_norm, c - 1)
                nc.gpsimd.tensor_tensor(inv_std[:, b, :], var_eps[:, b, :], half_neg[:, :], ALU.pow).then_inc(s_inv, 1)

            def near_step(i, b):
                if in_range(i, 2):
                    gather_src(i + 2, b, False)
                if in_range(i, -5):
                    inverse_std(i - 5, (b + 1) % 2)

            pool.wait_ge(s_near, 9)
            pool.wait_ge(s_guard, 1)
            with pool.If(pool.value_load(near[0:1, 0:1], min_val=0, max_val=1)):
                for b in range(NB):
                    gather_src(b, b, True)
                for i in range(PEEL):
                    near_step(i, i % 2)
                with pool.Fori(PEEL, LOOP_END, 2) as i0:
                    for b in range(2):
                        near_step(i0 + b, b)
                for i in range(LOOP_END, G + 5):
                    near_step(i, i % 2)
            with pool.Else():
                for b in range(NB):
                    gather(b, b, None)
                pool.wait_ge(s_init, 16 * (LC + 1))
                for b in range(NB):
                    scatter(b, b, b == 0)
                    gather(b + NB, b, b + 1)
                with pool.Fori(NB, G - NB, NB) as g0:
                    for b in range(NB):
                        scatter(g0 + b, b, False)
                        gather(g0 + (b + NB), b, g0 + (b + 1))
                for b in range(NB):
                    scatter(G - NB + b, b, False)
                pool.wait_ge(s_scq, 16 * T)
                pool.sem_inc(s_sc[0], 16 * TPG * (G // 2))
                pool.sem_inc(s_sc[1], 16 * TPG * (G // 2))

        @block.tensor
        def _(pe):
            pe.wait_ge(s_const, 8)
            pe.wait_ge(s_w, 16 * 9)
            nc.tensor.transpose(psA[0:D, 0:D], wue[:, :], ident[0:D, 0:D]).then_inc(s_wueT, 1)
            pe.wait_ge(s_wueTs, 1)
            nc.tensor.matmul(psB[0:D, 0:H], wueT[:, :], we1_low[:, :], start=True, stop=True).then_inc(s_fold, 1)
            pe.wait_ge(s_rawf, 1)
            for k, bank in ((0, psC), (1, psD)):
                for c in range(CH):
                    n = P if c < CH - 1 else TAIL_T
                    mm = nc.tensor.transpose(bank[:, c * P:c * P + n], rawf[0:n, k, c, :], ident[0:n, 0:n])
            mm.then_inc(s_idxT, 1)
            pe.wait_ge(s_rowv, 1)
            for row, bank in ((row_base, psT), (row_ali, psE), (row_span, psS)):
                for c in range(CH):
                    n = P if c < CH - 1 else TAIL_T
                    mm = nc.tensor.transpose(bank[0:1, c * P:c * P + n], row[0:n, c:c + 1], ident[0:n, 0:n])
            mm.then_inc(s_rowT, 1)
            pe.wait_ge(s_ali, 1)
            nc.tensor.matmul(psH[:, 0:T], ones[0:1, :], t_ali[0:1, :], start=True, stop=True).then_inc(s_alib, 1)
            pe.wait_ge(s_we, 2)
            pe.wait_ge(s_idx, 3)

            def transposes(g, b, round_, prior, tail=False):
                pe.wait_ge(s_eh[b], 16 * round_ + (16 if tail else 0))
                pe.wait_ge(s_gath[b], 16 * 2 * TPG * round_)
                for j in range(TPG):
                    mm = nc.tensor.transpose(psT[:, j * P:(j + 1) * P], xin[:, b, j, :], ident[:, :])
                mm.then_inc(s_T, 1)
                for j in range(TPG):
                    mm = nc.tensor.transpose(psH[0:D, j * P:(j + 1) * P], hd[:, b, j, :], ident[:, :])
                mm.then_inc(s_H, 1)

            def comb(g):
                pe.wait_ge(s_m12, g + 1)
                for j in range(TPG):
                    mm = nc.tensor.matmul(psE[:, j * D:(j + 1) * D], m12[:, j * P:(j + 1) * P], wc[:, :], start=True, stop=True)
                mm.then_inc(s_E, 1)

            def tile_sums(g, b, first=False):
                pe.wait_ge(s_same, g + 1)
                pe.wait_ge(s_msg, g + 1)
                if not first:
                    pe.wait_ge(s_tot, g)
                for j in range(TPG):
                    mm = nc.tensor.matmul(psS[:, j * D:(j + 1) * D], same[:, b, j, :], msg[:, j, :], start=True, stop=True)
                mm.then_inc(s_S, 1)

            def step(g, b, nxt_round, first=False, last=False, tail=False):
                pe.wait_ge(s_hsT, g + 1)
                nc.tensor.matmul(psA[:, :], w1[:, :], hsT[:, :], start=True, stop=True).then_inc(s_A, 1)
                if not first:
                    comb(g - 1)
                pe.wait_ge(s_ehT, g + 1)
                pe.wait_ge(s_prod, g + 1)
                nc.tensor.matmul(psC[:, :], we[:, :], peT[:, :], start=True, stop=True).then_inc(s_C, 1)
                if not first:
                    tile_sums(g - 1, (b + 1) % NB, first="g1" if False else False) if not (isinstance(g, int) and g == 1) else tile_sums(0, 0, True)
                if not last:
                    transposes(g + 1, (b + 1) % NB, nxt_round, None, tail)
                pe.wait_ge(s_r1, g + 1)
                nc.tensor.matmul(psB[:, :], w2[:, :], r1[:, :], start=True, stop=True).then_inc(s_B, 1)
                pe.wait_ge(s_r2, g + 1)
                nc.tensor.matmul(psD[:, :], we2[:, :], r2[:, :], start=True, stop=True).then_inc(s_D, 1)

            def pick_hd(g, b, round_):
                pe.wait_ge(s_pick, g + 1)
                pe.wait_ge(s_win[b], round_ * (16 * TPG))
                for j in range(TPG):
                    for k in range(WK):
                        for part in range(3):
                            mm = nc.tensor.matmul(psH[:, j * D:(j + 1) * D], pick[:, b, k, j * P:(j + 1) * P],
                                                  x_win[:, b, j, k, part * D:(part + 1) * D],
                                                  start=(k == 0 and part == 0), stop=(k == WK - 1 and part == 2))
                mm.then_inc(s_hd, 1)

            def turn_in(g, b):
                pe.wait_ge(s_prod, g + 1)
                for q in range(2):
                    nc.tensor.transpose(psH[:, (2 + q) * P:(3 + q) * P], hs[:, b, 2 * q:2 * q + 2, :].rearrange("p j d -> p (j d)"), ident[:, :])
                for j in range(TPG):
                    mm = nc.tensor.transpose(psT[:, j * P:(j + 1) * P], pe_in[:, b, j, :], ident[:, :])
                mm.then_inc(s_T, 1)

            def turn_out(g):
                pe.wait_ge(s_comb, g + 1)
                for j in range(TPG):
                    mm = nc.tensor.transpose(psE[:, j * P:(j + 1) * P], comb_sb[:, j * P:(j + 1) * P], ident[:, :])
                mm.then_inc(s_M, 1)

            def sum_messages(g, b):
                offs = [pe.value_load(t_off_i[0:1, bass.ds(g * TPG + j, 1)], min_val=0, max_val=SPAN * D) for j in range(TPG)]
                pe.wait_ge(s_putr, g + 1)
                pe.wait_ge(s_mlo, g + 1)
                if not isinstance(g, int) or g >= 1:
                    pe.wait_ge(s_add, g)
                nc.tensor.matmul(psS[:, 0:GB * D], zeros[:, 0:P], zeros[:, :], start=True, stop=False, skip_group_check=True)
                for j in range(TPG):
                    for k in range(OHB):
                        for n, part in enumerate((msg_hi, msg_lo)):
                            mm = nc.tensor.matmul(psS[:, bass.ds(offs[j] + k * D, D)], put[:, b, j, k * P:(k + 1) * P], part[:, j, :],
                                                  start=False, stop=(j == TPG - 1 and k == OHB - 1 and n == 1), skip_group_check=True)
                mm.then_inc(s_agg, 1)

            def near_step(i, b, next_round, edge_count):
                pe.wait_ge(s_hsP, i + 1)
                pairs = psA[:, :].rearrange("p (q r e) -> p q r e", q=2, r=2)
                cols = hsP[:, :].rearrange("p (q e) -> p q e", q=2)
                nc.tensor.matmul(pairs[:, :, 0, :], w1_even[:, :], cols, start=True, stop=True)
                nc.tensor.matmul(pairs[:, :, 1, :], w1_odd[:, :], cols, start=True, stop=True).then_inc(s_A, 1)
                if in_range(i, 1):
                    pick_hd(i + 1, (b + 1) % NB, next_round)
                pe.wait_ge(s_ehT, i + 1)
                nc.tensor.matmul(psC[:, :], we[:, :], peT[:, :], start=True, stop=True).then_inc(s_C, 1)
                if in_range(i, -1):
                    turn_out(i - 1)
                pe.wait_ge(s_r1, i + 1)
                nc.tensor.matmul(psB[:, :], w2[:, :], r1[:, :], start=True, stop=True).then_inc(s_B, 1)
                if in_range(i, 1):
                    pe.wait_ge(s_eh[(b + 1) % NB], edge_count)
                    turn_in(i + 1, (b + 1) % NB)
                pe.wait_ge(s_r2, i + 1)
                nc.tensor.matmul(psD[:, :], we2[:, :], r2[:, :], start=True, stop=True).then_inc(s_D, 1)
                if in_range(i, -1):
                    sum_messages(i - 1, (b + 1) % NB)
                pe.wait_ge(s_m12, i + 1)
                nc.tensor.matmul(psE[:, :], wc_wide[:, :], m12[:, :], start=True, stop=True).then_inc(s_E, 1)

            pe.wait_ge(s_near, 13)
            pe.wait_ge(s_guard, 1)
            with pe.If(pe.value_load(near[0:1, 0:1], min_val=0, max_val=1)):
                pick_hd(0, 0, 1)
                pe.wait_ge(s_eh[0], 16)
                turn_in(0, 0)
                near_step(0, 0, 1, 16)
                near_step(1, 1, 2, 32)
                with pe.Fori(1, G // 2 - 1) as k:
                    near_step(k * 2, 0, k + 1, k * 16 + 16)
                    near_step(k * 2 + 1, 1, k + 2, k * 16 + 32)
                near_step(G - 2, 0, G // 2, 16 * (G // 2) + 16)
                near_step(G - 1, 1, None, None)
                turn_out(G - 1)
                sum_messages(G - 1, 1)
            with pe.Else():
                transposes(0, 0, 1, None)
                step(0, 0, 1, first=True)
                step(1, 1, 2)
                with pe.Fori(1, G // NB - 1) as k:
                    step(k * NB, 0, k + 1)
                    step(k * NB + 1, 1, k + 2)
                step(G - 2, 0, G // NB, tail=True)
                step(G - 1, 1, None, last=True)
                comb(G - 1)
                tile_sums(G - 1, 1)

        @block.scalar
        def _(act):
            act.wait_ge(s_wueT, 1)
            nc.scalar.activation(wueT[:, :], psA[0:D, 0:D], ACT.Copy).then_inc(s_wueTs, 1)
            act.wait_ge(s_fold, 1)
            nc.scalar.activation(we[0:D, :], psB[0:D, 0:H], ACT.Copy, scale=0.2).then_inc(s_we, 1)
            act.wait_ge(s_w, 16 * 9)
            nc.scalar.activation(we[D:P, :], we[D:P, :], ACT.Copy, scale=0.8).then_inc(s_we, 1)

            def evacuate(g):
                act.wait_ge(s_T, g + 1)
                nc.scalar.activation(hsT[:, :], psT[0:D, :], ACT.Copy).then_inc(s_hsT, 1)
                nc.scalar.activation(peT[D:P, :], psT[D:P, :], ACT.Copy).then_inc(s_ehT, 1)

            def tanh(g):
                act.wait_ge(s_E, g + 1)
                nc.scalar.activation(msg[:, :, :].rearrange("p j d -> p (j d)"), psE[:, 0:TPG * D], ACT.Tanh).then_inc(s_msg, 1)

            def step(g, first=False, last=False):
                act.wait_ge(s_A, g + 1)
                nc.scalar.activation(r1[:, :], psA[:, :], ACT.Relu, bias=b1[:, 0:1]).then_inc(s_r1, 1)
                if not first:
                    tanh(g - 1)
                act.wait_ge(s_C, g + 1)
                nc.scalar.activation(r2[:, :], psC[:, :], ACT.Relu, bias=be1[:, 0:1]).then_inc(s_r2, 1)
                if not last:
                    evacuate(g + 1)
                act.wait_ge(s_B, g + 1)
                nc.scalar.activation(m1[:, :], psB[:, :], ACT.Copy).then_inc(s_m1, 1)

            act.wait_ge(s_near, 9)
            nc.scalar.activation(w1_even[0:D, :], w1[:, :], ACT.Copy).then_inc(s_near, 1)
            act.dma_start(w1_odd[D:P, :], w_n1).then_inc(s_w1o, 16)
            act.wait_ge(s_w1o, 16)
            nc.scalar.activation(wc_wide[:, 0:D], wc[:, :], ACT.Copy).then_inc(s_near, 3)

            def src_copy(g, b, gathers):
                if gathers is not None:
                    act.wait_ge(s_gath[b], gathers)
                nc.scalar.activation(src_now[:, b, :].rearrange("p (a j) -> p a j", a=1), idx[:, bass.ds(g, 1), 0:TPG], ACT.Copy).then_inc(s_srcn, 1)

            def high_part(c, b, loads, stores):
                act.wait_ge(s_xin[b], loads)
                if stores is not None:
                    act.wait_ge(s_xst[b], stores)
                nc.scalar.activation(x_split[:, b, :, 0:D], x_in[:, b, :, :], ACT.Copy).then_inc(s_hi, 1)
                nc.scalar.activation(nodes[:, bass.ds(c * CW, CW)], x_in[:, b, :, :].rearrange("p b d -> p (b d)"), ACT.Copy, scale=2.0).then_inc(s_two, 1)

            def middle_part(c, b):
                act.wait_ge(s_rest, c + 1)
                nc.scalar.activation(x_split[:, b, :, D:2 * D], x_rest[:, b, :, :], ACT.Copy).then_inc(s_mid, 1)

            def copy_in(g):
                act.wait_ge(s_T, g + 1)
                nc.scalar.activation(hsP[:, :], psH[:, 2 * P:4 * P], ACT.Copy).then_inc(s_hsP, 1)
                nc.scalar.activation(peT[:, :], psT[:, :], ACT.Copy).then_inc(s_ehT, 1)

            def near_tanh(g):
                act.wait_ge(s_M, g + 1)
                nc.scalar.activation(msg[:, :, :], psE[:, :].rearrange("p (j f) -> p j f", f=P)[:, :, 0:D], ACT.Tanh).then_inc(s_tanh, 1)
                act.wait_ge(s_tanh, g + 1)
                nc.scalar.activation(msg_hi[:, :, :], msg[:, :, :], ACT.Copy, scale=SCALE).then_inc(s_mhi, 1)

            def near_step(i, b, half):
                act.wait_ge(s_A, i + 1)
                nc.scalar.activation(r1[:, :], psA[:, :], ACT.Relu, bias=b1[:, 0:1]).then_inc(s_r1, 1)
                if in_range(i, 2):
                    src_copy(i + 2, b, (half + 1) * (16 * TPG))
                act.wait_ge(s_C, i + 1)
                nc.scalar.activation(r2[:, :], psC[:, :], ACT.Relu, bias=be1[:, 0:1]).then_inc(s_r2, 1)
                if in_range(i, -1):
                    near_tanh(i - 1)
                act.wait_ge(s_B, i + 1)
                nc.scalar.activation(m1[:, :], psB[:, :], ACT.Copy).then_inc(s_m1, 1)
                if in_range(i, 1):
                    copy_in(i + 1)
                if in_range(i, PRE):
                    loads = half * 16 + 16 * (PRE // 2 + 1)
                    if isinstance(i, int) and i + PRE == G - 1:
                        loads = loads + 16
                    high_part(i + PRE, b, loads, half * 16 + 16 * (PRE // 2))
                if in_range(i, PRE - 1):
                    middle_part(i + (PRE - 1), (b + 1) % 2)
                act.wait_ge(s_E, i + 1)
                nc.scalar.activation(comb_sb[:, :], psE[:, :], ACT.Copy).then_inc(s_comb, 1)

            act.wait_ge(s_idx, 3)
            act.wait_ge(s_guard, 1)
            with act.If(act.value_load(near[0:1, 0:1], min_val=0, max_val=1)):
                for b in range(NB):
                    src_copy(b, b, None)
                for c in range(PRE):
                    high_part(c, c % 2, 16 * (c // 2 + 1), None if c < 2 else 16 * (c // 2))
                    if c >= 1:
                        middle_part(c - 1, (c - 1) % 2)
                copy_in(0)
                for i in range(2):
                    near_step(i, i % 2, i // 2)
                with act.Fori(1, LOOP_END // 2) as k:
                    for b in range(2):
                        near_step(k * 2 + b, b, k)
                for i in range(LOOP_END, G):
                    near_step(i, i % 2, i // 2)
                near_tanh(G - 1)
            with act.Else():
                for c in range(LC):
                    act.wait_ge(s_xl[c % 2], 16 * (c // 2 + 1) + (16 if c == LC - 1 else 0))
                    nc.scalar.activation(nodes[:, c * LW:(c + 1) * LW], nodes[:, c * LW:(c + 1) * LW], ACT.Copy, scale=2.0).then_inc(s_two, 1)
                evacuate(0)
                step(0, first=True)
                with act.Fori(1, G - 1) as g:
                    step(g)
                step(G - 1, last=True)
                tanh(G - 1)
                for c in range(LC + 1):
                    if c < LC:
                        act.wait_ge(s_cent, c + 1)
                        if c >= 2:
                            act.wait_ge(s_ssq, c - 1)
                        nc.scalar.activation(sq[:, c % 2, :], nodes[:, c * LW:(c + 1) * LW], ACT.Square).then_inc(s_sq, 1)
                    if c >= 1:
                        act.wait_ge(s_ssq, c)
                        nc.scalar.activation(std[:, (c - 1) % 2, :], ssq[:, (c - 1) % 2, :], ACT.Sqrt, bias=eps[:, 0:1], scale=1.0 / D).then_inc(s_std, 1)

        @block.vector
        def _(dve):
            chain = [0]

            def link(ins):
                chain[0] += 1
                ins.then_inc(s_v, 1)
                dve.wait_ge(s_v, chain[0])

            nc.vector.memset(nodes[:, (B - 1) * D:B * D], 0.0).then_inc(s_lastz, 1)
            nc.vector.memset(w1_even[D:P, :], 0.0).then_inc(s_near, 1)
            nc.vector.memset(w1_odd[0:D, :], 0.0).then_inc(s_near, 1)
            link(nc.vector.memset(raw[:, 0, CH - 1, :], 0))
            nc.vector.memset(raw[:, 1, CH - 1, :], N).then_inc(s_pad, 1)
            dve.wait_ge(s_raw, 16 * 6)
            dve.wait_ge(s_pad, 1)
            nc.vector.tensor_copy(rawf[:, :, :, :].rearrange("p k c t -> p (k c t)"), raw[:, :, :, :].rearrange("p k c t -> p (k c t)")).then_inc(s_rawf, 1)
            steps = [0]

            def step_row(*ins):
                for i in ins:
                    steps[0] += 1
                    i.then_inc(s_row, 1)
                dve.wait_ge(s_row, steps[0])

            dve.wait_ge(s_rawf, 1)
            step_row(nc.vector.tensor_reduce(row_min[:, :], rawf[:, 1, :, :], AX_X, ALU.min),
                     nc.vector.tensor_scalar(same[:, 0, :, :], rawf[:, 1, :, :], float(N - 1), None, ALU.min))
            step_row(nc.vector.tensor_reduce(row_max[:, :], same[:, 0, :, :], AX_X, ALU.max),
                     nc.vector.tensor_scalar(row_base[:, :], row_min[:, :], float(N - WIN), None, ALU.min),
                     nc.vector.tensor_copy(row_mini[:, :], row_min[:, :]))
            step_row(nc.vector.tensor_tensor(row_span[:, :], row_max[:, :], row_base[:, :], ALU.subtract),
                     nc.vector.tensor_scalar(row_alii[:, :], row_mini[:, :], (1 << 20) - P, None, ALU.bitwise_and))
            step_row(nc.vector.tensor_copy(row_ali[:, :], row_alii[:, :]))
            for c in range(CH):
                i = nc.vector.tensor_scalar(row_loc[:, c, :], rawf[:, 1, c, :], row_base[:, c:c + 1], 1000.0, ALU.subtract, ALU.min)
            i.then_inc(s_rowv, 1)
            dve.wait_ge(s_rowT, 1)
            nc.vector.tensor_copy(t_ali[:, :], psE[0:1, 0:T]).then_inc(s_ali, 1)
            dve.wait_ge(s_ali, 1)
            step_row(nc.vector.tensor_copy(t_base_i[:, :], psT[0:1, 0:T]),
                     nc.vector.tensor_reduce(worst[:, 0:1], psS[0:1, 0:T], AX_X, ALU.max),
                     nc.vector.tensor_reduce(g_ali[:, :], psE[0:1, 0:T].rearrange("a (g j) -> a g j", j=TPG), AX_X, ALU.min))
            step_row(nc.vector.tensor_tensor(t_off[:, :].rearrange("a (g j) -> a g j", j=TPG), t_ali[:, :].rearrange("a (g j) -> a g j", j=TPG),
                                             g_ali[:, :].rearrange("a (g j) -> a g j", j=1).to_broadcast([1, G, TPG]), ALU.subtract),
                     nc.vector.tensor_scalar(g_col_i[:, :], g_ali[:, :], float(D) / P, None, ALU.mult))
            dve.wait_ge(s_const, 8)
            step_row(nc.vector.tensor_tensor(g_dev[:, :], g_ali[:, :], g_start[:, :], ALU.subtract),
                     nc.vector.tensor_reduce(worst[:, 1:2], t_off[:, :], AX_X, ALU.max),
                     nc.vector.tensor_scalar(t_off_i[:, :], t_off[:, :], float(D) / P, None, ALU.mult))
            step_row(nc.vector.tensor_reduce(worst[:, 2:3], g_dev[:, :], AX_X, ALU.max),
                     nc.vector.tensor_reduce(worst[:, 3:4], g_dev[:, :], AX_X, ALU.min))
            step_row(nc.vector.tensor_scalar(excess[:, 0:1], worst[:, 0:1], float(WIN - 1), None, ALU.subtract),
                     nc.vector.tensor_scalar(excess[:, 1:2], worst[:, 1:2], float(SPAN * P), None, ALU.subtract),
                     nc.vector.tensor_scalar(excess[:, 2:3], worst[:, 2:3], float(NEAR * P), None, ALU.subtract),
                     nc.vector.tensor_scalar(excess[:, 3:4], worst[:, 3:4], -1.0, float(NEAR * P), ALU.mult, ALU.subtract))
            step_row(nc.vector.tensor_reduce(most[:, :], excess[:, :], AX_X, ALU.max))
            nc.vector.tensor_scalar(near[:, :], most[:, :], 0.0, None, ALU.is_le).then_inc(s_guard, 1)
            dve.wait_ge(s_idxT, 1)
            idx4 = idx[:, :, :]
            nc.vector.tensor_copy(idx4[:, :, 0:TPG], psC[:, 0:T].rearrange("p (g j) -> p g j", j=TPG)).then_inc(s_idx, 1)
            nc.vector.tensor_scalar(idx4[:, :, TPG:2 * TPG], psD[:, 0:T].rearrange("p (g j) -> p g j", j=TPG), float(N - 1), None, ALU.min).then_inc(s_idx, 1)
            nc.vector.tensor_copy(dstf[:, :], psD[:, 0:T]).then_inc(s_idx, 1)
            dve.wait_ge(s_idx, 3)
            dve.wait_ge(s_const, 8)
            link(nc.vector.tensor_tensor(spare[:, :], spare[:, :], dstf[:, :], ALU.subtract))

            dve.wait_ge(s_alib, 1)
            nc.vector.tensor_tensor(dst_in_block[:, :], dstf[:, :], psH[:, 0:T], ALU.subtract).then_inc(s_near, 1)
            dve.wait_ge(s_near, 14)

            def make_pick(g, b, round_):
                dve.wait_ge(s_dwin[b], round_ * 16)
                if not isinstance(g, int) or g >= NB:
                    dve.wait_ge(s_hd, g - (NB - 1))
                for k in range(WK):
                    i = nc.vector.tensor_scalar(pick[:, b, k, :], dst_win[:, b, :], win_at[:, k:k + 1], None, ALU.is_equal)
                i.then_inc(s_pick, 1)

            def make_put(g, b):
                if not isinstance(g, int) or g >= NB:
                    dve.wait_ge(s_agg, g - (NB - 1))
                for j in range(TPG):
                    i = nc.vector.tensor_scalar(put[:, b, j, :], block_at[:, :], dst_in_block[:, bass.ds(g * TPG + j, 1)], None, ALU.is_equal)
                i.then_inc(s_putr, 1)

            def near_product(g, b, gathers):
                dve.wait_ge(s_gath[b], gathers)
                dve.wait_ge(s_hd, g + 1)
                nc.vector.tensor_tensor(pe_in[:, b, :, 0:D], psH[:, 0:TPG * D].rearrange("p (j d) -> p j d", d=D), hs[:, b, :, :], ALU.mult).then_inc(s_prod, 1)

            def low_message(g):
                dve.wait_ge(s_mhi, g + 1)
                nc.vector.scalar_tensor_tensor(out=msg_lo[:, :, :], in0=msg[:, :, :], scalar=SCALE, in1=msg_hi[:, :, :],
                                               op0=ALU.mult, op1=ALU.subtract).then_inc(s_mlo, 1)

            def add_sums(g, chunks):
                col = dve.value_load(g_col_i[0:1, bass.ds(g, 1)], min_val=0, max_val=(B - 1) * D)
                dve.wait_ge(s_agg, g + 1)
                dve.wait_ge(s_two, chunks)
                nc.vector.scalar_tensor_tensor(out=nodes[:, bass.ds(col, GB * D)], in0=psS[:, 0:GB * D], scalar=1.0 / SCALE,
                                               in1=nodes[:, bass.ds(col, GB * D)], op0=ALU.mult, op1=ALU.add).then_inc(s_add, 1)

            def rest_part(c, b):
                dve.wait_ge(s_hi, c + 1)
                nc.vector.tensor_tensor(x_rest[:, b, :, :], x_in[:, b, :, :], x_split[:, b, :, 0:D], ALU.subtract).then_inc(s_rest, 1)

            def low_part(c, b):
                dve.wait_ge(s_mid, c + 1)
                nc.vector.tensor_tensor(x_split[:, b, :, 2 * D:3 * D], x_rest[:, b, :, :], x_split[:, b, :, D:2 * D], ALU.subtract).then_inc(s_low, 1)

            def chunk_stats(c, b):
                for k in range(CB):
                    i = nc.vector.bn_stats(stats[:, b, k, :], nodes[:, bass.ds(c * CW + k * D, D)])
                i.then_inc(s_stats, 1)

            def chunk_mean_var(c, b):
                for k in range(CB):
                    i = nc.vector.bn_aggr(mv[:, b, k, :], stats[:, b, k, :])
                i.then_inc(s_mv, 1)

            def add_eps(c, b):
                dve.wait_ge(s_mv, c + 1)
                nc.vector.tensor_scalar(var_eps[:, b, :], mv[:, b, :, 1], 1e-5, None, ALU.add).then_inc(s_eps, 1)

            def normalise(c, b):
                dve.wait_ge(s_inv, c + 1)
                for k in range(CB):
                    here = nodes[:, bass.ds(c * CW + k * D, D)]
                    i = nc.vector.tensor_scalar(here, here, mv[:, b, k, 0:1], inv_std[:, b, k:k + 1], ALU.subtract, ALU.mult)
                i.then_inc(s_norm, 1)

            def near_step(i, b, half):
                o = (b + 1) % 2
                if in_range(i, 1):
                    near_product(i + 1, o, (half + 1 + b) * (16 * TPG))
                if in_range(i, 2):
                    make_pick(i + 2, b, half + 2)
                if in_range(i, 0):
                    make_put(i, b)
                if in_range(i, -1):
                    low_message(i - 1)
                if in_range(i, -6):
                    normalise(i - 6, b)
                if in_range(i, -4):
                    dve.wait_ge(s_stats, i - 3)
                    if in_range(i, -6):
                        dve.wait_ge(s_norm, i - 5)
                if in_range(i, 0):
                    dve.wait_ge(s_D, i + 1)
                    dve.wait_ge(s_m1, i + 1)
                    nc.vector.tensor_tensor(m12[:, :], psD[:, :], m1[:, :], ALU.mult).then_inc(s_m12, 1)
                if in_range(i, -4):
                    chunk_mean_var(i - 4, b)
                if in_range(i, PRE - 1):
                    low_part(i + (PRE - 1), o)
                if in_range(i, -4):
                    add_eps(i - 4, b)
                if in_range(i, -1):
                    add_sums(i - 1, min(i + 3, G) if isinstance(i, int) else i + 3)
                    dve.wait_ge(s_add, i)
                if in_range(i, PRE):
                    rest_part(i + PRE, b)
                if in_range(i, -3):
                    chunk_stats(i - 3, o)

            with dve.If(dve.value_load(near[0:1, 0:1], min_val=0, max_val=1)):
                for c in range(PRE):
                    rest_part(c, c % 2)
                    if c >= 1:
                        low_part(c - 1, (c - 1) % 2)
                for b in range(NB):
                    make_pick(b, b, 1)
                near_product(0, 0, 16 * TPG)
                for i in range(PEEL):
                    near_step(i, i % 2, i // 2)
                with dve.Fori(PEEL // 2, LOOP_END // 2) as k:
                    for b in range(2):
                        near_step(k * 2 + b, b, k)
                for i in range(LOOP_END, G + 6):
                    near_step(i, i % 2, i // 2)

            def indices(g, b, prior):
                if prior is not None:
                    dve.wait_ge(s_gath[b], prior)
                nc.vector.tensor_copy(idx_now[:, b, :].rearrange("p (a j) -> p a j", a=1), idx[:, bass.ds(g, 1), :]).then_inc(s_idxn, 1)

            def product(g):
                dve.wait_ge(s_H, g + 1)
                dve.wait_ge(s_hsT, g + 1)
                nc.vector.tensor_tensor(peT[0:D, :], psH[0:D, :], hsT[:, :], ALU.mult).then_inc(s_prod, 1)

            VC = 3
            V0 = chain[0]

            def equal_dst(g, b, round_, prior):
                dve.wait_ge(s_dstb[b], 16 * round_)
                for j in range(TPG):
                    i = nc.vector.tensor_scalar(same[:, b, j, :], dst_all[:, b, j * P:(j + 1) * P],
                                            dstf[:, bass.ds(g * TPG + j, 1)], None, ALU.is_equal)
                i.then_inc(s_same, 1)
                dve.wait_ge(s_same, g + 1)
                for j in range(TPG):
                    i = nc.vector.tensor_tensor_reduce(junk[:, j, :], same[:, b, j, :], lower[:, :], 1.0, 0.0, ALU.mult, ALU.add, earlier[:, j:j + 1])
                i.then_inc(s_v, 1)
                dve.wait_ge(s_v, g * VC + (V0 + 1))
                nc.vector.tensor_scalar(dup[:, :], earlier[:, :], 1.0, None, ALU.min).then_inc(s_v, 1)
                dve.wait_ge(s_v, g * VC + (V0 + 2))
                nc.vector.tensor_tensor(moved[:, :], dup[:, :], spare[:, bass.ds(g * TPG, TPG)], ALU.mult).then_inc(s_v, 1)
                dve.wait_ge(s_v, g * VC + (V0 + 3))
                if prior is not None:
                    dve.wait_ge(s_scq, prior * (16 * TPG))
                nc.vector.tensor_tensor(put_at[:, b, :], moved[:, :], dstf[:, bass.ds(g * TPG, TPG)], ALU.add).then_inc(s_put, 1)

            def totals(g, b, prior):
                dve.wait_ge(s_S, g + 1)
                if prior is not None:
                    dve.wait_ge(s_scq, prior * (16 * TPG))
                nc.vector.tensor_copy(tot[:, b, :, :].rearrange("p j d -> p (j d)"), psS[:, 0:TPG * D]).then_inc(s_tot, 1)

            def step(g, b, round_, first=False, last=False, peeled=False):
                pr = None if peeled else g - (NB - 1)
                if not last:
                    indices(g + NB, b, round_ * (16 * 2 * TPG)) if not last else None
                equal_dst(g, b, round_, pr)
                if not first:
                    totals(g - 1, (b + 1) % NB, None if (peeled) else g - NB)
                product(g + 1)
                dve.wait_ge(s_D, g + 1)
                dve.wait_ge(s_m1, g + 1)
                nc.vector.tensor_tensor(m12[:, :], psD[:, :], m1[:, :], ALU.mult).then_inc(s_m12, 1)

            def step_end(g, b, round_, more):
                equal_dst(g, b, round_, g - (NB - 1))
                totals(g - 1, (b + 1) % NB, g - NB)
                if more:
                    product(g + 1)
                dve.wait_ge(s_D, g + 1)
                dve.wait_ge(s_m1, g + 1)
                nc.vector.tensor_tensor(m12[:, :], psD[:, :], m1[:, :], ALU.mult).then_inc(s_m12, 1)

            with dve.Else():
                for b in range(NB):
                    indices(b, b, None)
                product(0)
                step(0, 0, 1, first=True, peeled=True)
                step(1, 1, 1, peeled=True)
                with dve.Fori(1, G // NB - 1) as k:
                    step(k * NB, 0, k + 1)
                    step(k * NB + 1, 1, k + 1)
                step_end(G - 2, 0, G // NB, True)
                step_end(G - 1, 1, G // NB, False)
                totals(G - 1, 1, G - NB)

                dve.wait_ge(s_back, 16 * (LC + 1))
                def scale_out(c):
                    dve.wait_ge(s_std, c + 1)
                    nc.vector.reciprocal(rstd[:, c % 2, :], std[:, c % 2, :]).then_inc(s_ln, 1)
                    ln[0] += 1
                    dve.wait_ge(s_ln, ln[0])
                    nc.vector.tensor_tensor(node_chunk(c), node_chunk(c), rstd[:, c % 2, :].rearrange("p (b a) -> p b a", a=1).to_broadcast([P, LN_BLOCKS, D]), ALU.mult).then_inc(s_norm, 1)

                ln = [0]
                for c in range(LC + 1):
                    if c < LC:
                        nc.vector.tensor_reduce(mean[:, c % 2, :], node_chunk(c), AX_X, ALU.add).then_inc(s_ln, 1)
                        ln[0] += 1
                        dve.wait_ge(s_ln, ln[0])
                        nc.vector.tensor_scalar(nmean[:, c % 2, :], mean[:, c % 2, :], 1.0 / D, None, ALU.mult).then_inc(s_ln, 1)
                        ln[0] += 1
                        dve.wait_ge(s_ln, ln[0])
                        nc.vector.tensor_tensor(node_chunk(c), node_chunk(c), nmean[:, c % 2, :].rearrange("p (b a) -> p b a", a=1).to_broadcast([P, LN_BLOCKS, D]), ALU.subtract).then_inc(s_cent, 1)
                    if c >= 1:
                        scale_out(c - 1)
                    if c < LC:
                        dve.wait_ge(s_sq, c + 1)
                        if c >= 2:
                            dve.wait_ge(s_std, c - 1)
                        nc.vector.tensor_reduce(ssq[:, c % 2, :], sq[:, c % 2, :].rearrange("p (b d) -> p b d", d=D), AX_X, ALU.add).then_inc(s_ssq, 1)


_INS = ['x', 'src', 'dst', 'edge_attr_64', 'L0_gnn_W_node1', 'L0_gnn_b_node1', 'L0_gnn_W_node2', 'L0_gnn_W_edge1',
        'L0_gnn_b_edge1', 'L0_gnn_W_edge2', 'L0_gnn_W_comb', 'L0_gnn_W_ue']


def kernel(**inputs):
    import numpy as _np
    import concourse.bacc as _bacc
    from concourse import mybir as _mybir
    from concourse.bass_utils import run_bass_kernel_spmd as _run

    nc = _bacc.Bacc("TRN2", target_bir_lowering=False, num_devices=1)
    arrays, args = {}, []
    for name in _INS:
        a = _np.ascontiguousarray(inputs[name])
        arrays[f"in_{name}_dram"] = a
        args.append(nc.dram_tensor(f"in_{name}_dram", a.shape, _mybir.dt.from_np(a.dtype), kind="ExternalInput").ap())
    args.append(nc.dram_tensor("out_dram", (50000, 64), _mybir.dt.float32, kind="ExternalOutput").ap())
    gnn_kernel(nc, *args)
    r = _run(nc, [arrays], core_ids=[0])
    return r.results[0]["out_dram"]
```

```python
from contextlib import ExitStack

import concourse.bass as bass
from concourse import mybir

P = 128
F32 = mybir.dt.float32
I32 = mybir.dt.int32
F16 = mybir.dt.float16
BF16 = mybir.dt.bfloat16
ALU = mybir.AluOpType
ACT = mybir.ActivationFunctionType
AX_X = mybir.AxisListType.X

TPG = 4
NB = 2
LN_BLOCKS = 23

WK = 2
WIN = WK * P
GW = TPG + WK - 1
FRONT = 1
BACK = 2
TILE_FIRST = (0, 0, 1, 2)
TILE_END = (3, 4, 5, 6)
TILE_SPAN = 3
OHB = 4
GB = TILE_END[-1]
NEAR = 8
PRE = 8
SCALE = 4096.0


def gnn_kernel(nc, x, src, dst, eh, w_n1, b_n1, w_n2, w_e1, b_e1, w_e2, w_comb, w_ue, out):
    N, D = x.shape
    E = src.shape[0]
    H = w_n1.shape[1]
    G = -(-E // (P * TPG))
    T = G * TPG
    GE = P * TPG
    FULL_T = E // P
    TAIL_E = E - FULL_T * P
    assert G <= P
    B = -(-N // P)
    TAIL_N = N - (B - 1) * P
    LC = B // LN_BLOCKS
    assert LC * LN_BLOCKS == B and G % NB == 0 and D == 64 and H == P
    LW = LN_BLOCKS * D
    CB = TPG
    CW = CB * D
    TAIL_B = B - (G - 1) * CB
    assert -(-B // CB) == G and 0 < TAIL_B <= CB
    PAD_B = G * CB + GB + 1

    with ExitStack() as ctx:
        def sb(name, shape, dt=F32):
            return ctx.enter_context(nc.sbuf_tensor(name, shape, dt))

        def ps(name, shape, dt=F32):
            return ctx.enter_context(nc.psum_tensor(name, shape, dt))

        def sem(name):
            return ctx.enter_context(nc.semaphore(name))

        dst_rows = nc.dram_tensor("dst_rows", (T, P), F32, kind="Internal").ap()
        dst_local = nc.dram_tensor("dst_local", (T, P), F16, kind="Internal").ap()
        x_parts = nc.dram_tensor("x_parts", (FRONT * P + G * GE + BACK * P, 3 * D), BF16, kind="Internal").ap()
        sums = nc.dram_tensor("node_sums", (N + P, D), F32, kind="Internal").ap()

        ident = sb("ident", [P, P])
        lower = sb("lower", [P, P])
        w2 = sb("w2", [H, H])
        we = sb("we", [P, H])
        we1_low = sb("we1_low", [D, H])
        we2 = sb("we2", [H, H])
        wue = sb("wue", [D, D])
        wueT = sb("wueT", [D, D])
        b1 = sb("b1", [H, 1])
        be1 = sb("be1", [H, 1])
        eps = sb("eps", [P, 1])
        raw = sb("raw", [P, 2, TPG, P], I32)
        rawf = sb("rawf", [P, 2, TPG, P])
        idx = sb("idx", [P, G, 2 * TPG], I32)
        dstf = sb("dstf", [P, T])
        spare = sb("spare", [P, T])
        idx_now = sb("idx_now", [P, NB, 2 * TPG], I32)
        nodes = sb("nodes", [P, PAD_B * D])
        xin = sb("xin", [P, NB, TPG, 2 * D])
        hd = sb("hd", [P, NB, TPG, D])
        dst_all = sb("dst_all", [P, NB, GE])
        hsT = sb("hsT", [D, GE])
        peT = sb("peT", [P, GE])
        r1 = sb("r1", [H, GE])
        r2 = sb("r2", [H, GE])
        m1 = sb("m1", [H, GE])
        m12 = sb("m12", [H, GE])
        msg = sb("msg", [P, TPG, D])
        same = sb("same", [P, 2, TPG, P])
        junk = sb("junk", [P, TPG, P])
        earlier = sb("earlier", [P, TPG])
        dup = sb("dup", [P, TPG])
        moved = sb("moved", [P, TPG])
        put_at = sb("put_at", [P, 2, TPG], I32)
        tot = sb("tot", [P, 2, TPG, D])
        sq = sb("sq", [P, 2, LW])
        mean = sb("mean", [P, 2, LN_BLOCKS])
        nmean = sb("nmean", [P, 2, LN_BLOCKS])
        ssq = sb("ssq", [P, 2, LN_BLOCKS])
        std = sb("std", [P, 2, LN_BLOCKS])
        rstd = sb("rstd", [P, 2, LN_BLOCKS])

        tile_start = sb("tile_start", [P, TPG])
        tile_end = sb("tile_end", [P, TPG])
        tile_first = sb("tile_first", [P, TPG])
        g_start = sb("g_start", [P, 1])
        row_min = sb("row_min", [P, TPG])
        row_max = sb("row_max", [P, TPG])
        row_mini = sb("row_mini", [P, TPG], I32)
        row_alii = sb("row_alii", [P, TPG], I32)
        row_rel = sb("row_rel", [P, 4, TPG])
        low = sb("low", [P, 1])
        g_ali = sb("g_ali", [P, 1])
        g_base = sb("g_base", [P, 1])
        row_first = sb("row_first", [P, TPG])
        row_base = sb("row_base", [P, TPG])
        row_last = sb("row_last", [P, 2])
        excess = sb("excess", [P, 6])
        told = sb("told", [P, 3])
        row_loc = sb("row_loc", [P, TPG, P], F16)
        most = sb("most", [1, 1])
        near = sb("near", [1, 1], I32)
        g_base_i = sb("g_base_i", [1, G], I32)
        g_col_i = sb("g_col_i", [1, G], I32)
        w1_even = sb("w1_even", [P, H])
        w1_odd = sb("w1_odd", [P, H])
        wc_wide = sb("wc_wide", [H, P])
        win_at = sb("win_at", [P, WK])
        zeros = sb("zeros", [P, 3 * D], BF16)
        block_at = sb("block_at", [P, OHB * P], F16)
        half_neg = sb("half_neg", [P, CB])
        dst_in_block = sb("dst_in_block", [P, T])
        hs = hd
        pe_in = xin
        src_now = sb("src_now", [P, NB, TPG], I32)
        x_win = sb("x_win", [P, NB, GW, 3 * D], BF16)
        dst_win = sb("dst_win", [P, NB, GE], F16)
        pick = sb("pick", [P, NB, WK, GE], BF16)
        put = sb("put", [P, NB, TPG, OHB * P], F16)
        hsP = sb("hsP", [P, 2 * P])
        ident16 = sb("ident16", [P, P], F16)
        msgT = dst_all[:, 0, :]
        msgT_parts = sb("msgT_parts", [P, GE], F16)
        msg_parts = sb("msg_parts", [P, TPG, 2 * D], F16)
        x_in = junk[:, :, :].rearrange("p (n a) (h d) -> p n (a h) d", n=2, h=2)
        x_rest = tot
        x_split_first = sb("x_split_first", [P, 2, PRE // 2 * CB, 3 * D], BF16)
        x_split = sb("x_split", [P, 2, CB, 3 * D], BF16)
        stats = sb("stats", [P, 2, CB, 6])
        mv = sb("mv", [P, 2, CB, 2])
        var_eps = sb("var_eps", [P, 2, CB])
        inv_std = sb("inv_std", [P, 2, CB])

        psT = ps("psT", [P, GE])
        psH = ps("psH", [P, GE])
        psA = ps("psA", [P, GE])
        psB = ps("psB", [P, GE])
        psC = ps("psC", [P, GE])
        psD = ps("psD", [P, GE])
        psE = ps("psE", [P, GE])
        psS = ps("psS", [P, GE])

        s_const = sem("constants_made")
        s_w = sem("weights_loaded")
        s_pad = sem("index_pads_set")
        s_raw = [sem(f"raw_{name}_loaded") for name in ("src", "dst")]
        s_rawf = sem("raw_indices_float")
        s_dstrow = sem("dst_rows_stored")
        s_idxT = sem("indices_transposed")
        s_idx = sem("indices_ready")
        s_wueT = sem("wue_transposed")
        s_wueTs = sem("wue_copied")
        s_fold = sem("fold_multiplied")
        s_we = sem("edge_weights_ready")
        s_xl = [sem(f"x_loaded{i}") for i in range(2)]
        s_lastz = sem("last_block_cleared")
        s_two = sem("nodes_doubled")
        s_init = sem("sums_initialised")
        s_back = sem("sums_back")
        s_gath = [sem(f"rows_gathered{b}") for b in range(NB)]
        s_eh = [sem(f"edges_loaded{b}") for b in range(NB)]
        s_dstb = [sem(f"dst_broadcast{b}") for b in range(NB)]
        s_idxn = sem("idx_now_ready")
        s_T = sem("transposes_done")
        s_H = sem("hd_transposed")
        s_hsT = sem("hsT_ready")
        s_ehT = sem("ehT_ready")
        s_prod = sem("product_ready")
        s_A = sem("node1_done")
        s_B = sem("node2_done")
        s_C = sem("edge1_done")
        s_D = sem("edge2_done")
        s_E = sem("comb_done")
        s_S = sem("tile_sums_done")
        s_r1 = sem("relu_node_ready")
        s_r2 = sem("relu_edge_ready")
        s_m1 = sem("m1_copied")
        s_m12 = sem("m12_ready")
        s_msg = sem("messages_ready")
        s_same = sem("same_ready")
        s_tot = sem("totals_ready")
        s_put = sem("put_at_ready")
        s_v = sem("vector_chain")
        s_scq = sem("tiles_scattered")
        s_ln = sem("norm_chain")
        s_cent = sem("centred")
        s_sq = sem("squared")
        s_ssq = sem("squares_summed")
        s_std = sem("std_ready")
        s_norm = sem("normalised")
        s_out = sem("stored")

        s_row = sem("row_chain")
        s_rowv = sem("row_values_ready")
        s_local = sem("dst_local_stored")
        s_dinb = sem("dst_in_block_ready")
        s_rowT = sem("row_values_transposed")
        s_inb = sem("dst_in_block_rows_ready")
        s_inbT = sem("dst_in_block_transposed")
        s_told = sem("row_results_ready")
        s_xfirst = [sem(f"first_x_loaded{n}") for n in range(2)]
        s_xfst = [sem(f"first_x_parts_stored{n}") for n in range(3)]
        s_xpad = sem("x_parts_pads_stored")
        s_guard = sem("guard_ready")
        s_near = sem("near_constants_ready")
        s_xin = [sem(f"x_chunk_loaded{b}") for b in range(2)]
        s_hi = sem("x_high_ready")
        s_rest = sem("x_rest_ready")
        s_mid = sem("x_middle_ready")
        s_low = sem("x_low_ready")
        s_xst = [sem(f"x_parts_stored{b}") for b in range(2)]
        s_win = [sem(f"windows_loaded{b}") for b in range(NB)]
        s_dwin = [sem(f"window_dst_loaded{b}") for b in range(NB)]
        s_srcn = sem("src_now_ready")
        s_pick = sem("pick_ready")
        s_hd = sem("hd_picked")
        s_putr = sem("put_ready")
        s_hsP = sem("hsP_ready")
        s_M = sem("messages_transposed")
        s_msgs = sem("message_parts_copied")
        s_tanh = sem("tanh_ready")
        s_mhi = sem("message_high_ready")
        s_mlo = sem("message_low_ready")
        s_agg = sem("group_summed")
        s_add = sem("sums_added")
        s_stats = sem("stats_ready")
        s_mv = sem("mean_var_ready")
        s_eps = sem("eps_added")
        s_inv = sem("inverse_std_ready")

        block = ctx.enter_context(nc.Block())

        def x_chunk(c):
            return x[c * LN_BLOCKS * P:(c + 1) * LN_BLOCKS * P, :].rearrange("(b p) d -> p b d", p=P)

        def node_chunk(c):
            return nodes[:, c * LW:(c + 1) * LW].rearrange("p (b d) -> p b d", d=D)

        N_FULL = (LN_BLOCKS - 1) * P
        LAST = (LC - 1) * LN_BLOCKS * P

        def move_last(eng, dram, to_dram, s):
            a = dram[LAST:LAST + N_FULL, :].rearrange("(b p) d -> p b d", p=P)
            sa = nodes[:, (LC - 1) * LW:(LC - 1) * LW + (LN_BLOCKS - 1) * D].rearrange("p (b d) -> p b d", d=D)
            t = dram[LAST + N_FULL:N, :]
            st = nodes[0:TAIL_N, (B - 1) * D:B * D]
            for u, v in ((a, sa), (t, st)):
                if to_dram:
                    eng.dma_start(u, v).then_inc(s, 16)
                else:
                    eng.dma_start(v, u).then_inc(s, 16)

        def first_x(n):
            return nodes[:, n * (PRE // 2) * CW:(n + 1) * (PRE // 2) * CW].rearrange("p (b d) -> p b d", d=D)

        def first_rest(n):
            return sq[:, n, 0:PRE // 2 * CW].rearrange("p (b d) -> p b d", d=D)

        PEEL = 12
        ACT_PEEL = 6
        LOOP_END = (G - PRE - 2) // 2 * 2
        OUT_LAG = 7

        def in_range(i, lag):
            return not isinstance(i, int) or 0 <= i + lag < G

        @block.sync
        def _(sp):
            sp.wait_ge(s_pad, 2)
            for k, a in ((1, dst), (0, src)):
                sp.dma_start(raw[0:G - 1, k, :, :], a[0:(G - 1) * GE].rearrange("(g j p) -> g j p", j=TPG, p=P)).then_inc(s_raw[k], 16)
                rest = E - (G - 1) * GE
                sp.dma_start(raw[G - 1:G, k, :, :].rearrange("a j p -> a (j p)")[:, 0:rest], a[(G - 1) * GE:E].rearrange("(a f) -> a f", a=1)).then_inc(s_raw[k], 16)
            for t, a in ((wue, w_ue), (we1_low, w_e1), (we[D:P, :], w_e1), (w1_even[0:D, :], w_n1), (w1_odd[D:P, :], w_n1), (w2, w_n2),
                         (we2, w_e2), (wc_wide[:, 0:D], w_comb), (wc_wide[:, D:P], w_comb),
                         (b1, b_n1.rearrange("(h a) -> h a", a=1)), (be1, b_e1.rearrange("(h a) -> h a", a=1))):
                sp.dma_start(t[:, :], a).then_inc(s_w, 16)
            sp.wait_ge(s_rowv, 1)
            sp.dma_start(dst_local.rearrange("(g j) p -> g j p", j=TPG), row_loc[0:G, :, :]).then_inc(s_local, 16)
            sp.wait_ge(s_local, 16)
            sp.wait_ge(s_xpad, 16 * (FRONT + BACK))
            sp.wait_ge(s_guard, 1)

            def load_x(c, b):
                if isinstance(c, int) and c == G - 1:
                    a = x[c * GE:c * GE + (TAIL_B - 1) * P, :].rearrange("(b p) d -> p b d", p=P)
                    sp.dma_start(x_in[:, b, 0:TAIL_B - 1, :], a).then_inc(s_xin[b], 16)
                    sp.dma_start(x_in[0:TAIL_N, b, TAIL_B - 1, :], x[(B - 1) * P:N, :]).then_inc(s_xin[b], 16)
                else:
                    sp.dma_start(x_in[:, b, :, :], x[bass.ds(c * GE, GE), :].rearrange("(b p) d -> p b d", p=P)).then_inc(s_xin[b], 16)

            def store_split(c, b):
                sp.wait_ge(s_low, c + 1)
                sp.dma_start(x_parts[bass.ds(c * GE + FRONT * P, GE), :].rearrange("(b p) d -> p b d", p=P), x_split[:, b, :, :]).then_inc(s_xst[b], 16)

            def load_dst(g, b, fresh):
                if not fresh:
                    sp.wait_ge(s_pick, g - (NB - 1))
                sp.dma_start(dst_win[:, b, :], dst_local.rearrange("(g j) p -> g (j p)", j=TPG)[bass.ds(g, 1), :].to_broadcast([P, GE])).then_inc(s_dwin[b], 16)

            def load_group(g, b, fresh, stored0, stored1):
                if not fresh:
                    sp.wait_ge(s_hd, g - (NB - 1))
                for s, stored in zip(s_xst, (stored0, stored1)):
                    if not isinstance(stored, int) or stored > 0:
                        sp.wait_ge(s, stored)
                first = sp.value_load(g_base_i[0:1, bass.ds(g, 1)], min_val=0, max_val=(FRONT + BACK - GW) * P + G * GE)
                sp.dma_start(x_win[:, b, :, :], x_parts[bass.ds(first, GW * P), :].rearrange("(m p) d -> p m d", p=P)).then_inc(s_win[b], 16)

            def store_out(c):
                sp.wait_ge(s_norm, c + 1)
                if isinstance(c, int) and c == G - 1:
                    a = out[c * GE:c * GE + (TAIL_B - 1) * P, :].rearrange("(b p) d -> p b d", p=P)
                    sp.dma_start(a, nodes[:, c * CW:c * CW + (TAIL_B - 1) * D].rearrange("p (b d) -> p b d", d=D)).then_inc(s_out, 16)
                    sp.dma_start(out[(B - 1) * P:N, :], nodes[0:TAIL_N, (B - 1) * D:B * D]).then_inc(s_out, 16)
                else:
                    sp.dma_start(out[bass.ds(c * GE, GE), :].rearrange("(b p) d -> p b d", p=P),
                                 nodes[:, bass.ds(c * CW, CW)].rearrange("p (b d) -> p b d", d=D)).then_inc(s_out, 16)

            def near_step(i, b, half):
                if in_range(i, PRE - 2) and not (isinstance(i, int) and i < 2):
                    store_split(i + (PRE - 2), b)
                if in_range(i, 3):
                    load_dst(i + 3, (b + 1) % NB, False)
                if in_range(i, PRE + 1):
                    sp.wait_ge(s_rest, i + PRE)
                    sp.wait_ge(s_two, i + PRE)
                    load_x(i + (PRE + 1), (b + 1) % 2)
                if in_range(i, 2):
                    n = (half + (3 - PRE // 2)) * 16 if not isinstance(i, int) else None
                    s0 = n if n is not None else 16 * ((min(i + 5, G - 1)) // 2 + 1 - PRE // 2)
                    s1 = n if n is not None else 16 * ((min(i + 5, G - 1) + 1) // 2 - PRE // 2)
                    load_group(i + 2, b, False, s0, s1)
                if in_range(i, -OUT_LAG):
                    store_out(i - OUT_LAG)

            with sp.If(sp.value_load(near[0:1, 0:1], min_val=0, max_val=1)):
                load_x(PRE, 0)
                for b in range(NB):
                    load_dst(b, b, True)

                def store_first(c0, c1, s):
                    n, at = c0 // (PRE // 2), c0 % (PRE // 2) * CB
                    sp.wait_ge(s_low, c1)
                    sp.dma_start(x_parts[FRONT * P + c0 * GE:FRONT * P + c1 * GE, :].rearrange("(b p) d -> p b d", p=P),
                                 x_split_first[:, n, at:at + (c1 - c0) * CB, :]).then_inc(s, 16)

                store_first(0, PRE // 2, s_xfst[0])
                store_first(PRE // 2, PRE // 2 + 1, s_xfst[1])
                sp.wait_ge(s_xfst[0], 16)
                load_group(0, 0, True, 0, 0)
                store_first(PRE // 2 + 1, PRE, s_xfst[2])
                sp.wait_ge(s_xfst[1], 16)
                load_group(1, 1, True, 0, 0)
                sp.wait_ge(s_xfst[2], 16)
                load_dst(NB, 0, False)
                for i in range(PEEL):
                    near_step(i, i % 2, None)
                with sp.Fori(PEEL // 2, LOOP_END // 2) as k:
                    for b in range(2):
                        near_step(k * 2 + b, b, k)
                for i in range(LOOP_END, G + OUT_LAG):
                    near_step(i, i % 2, None)
                sp.wait_ge(s_out, 16 * (G + 1))
            with sp.Else():
                sp.dma_start(dst_rows.rearrange("(g j) p -> g j p", j=TPG), rawf[0:G, 1, :, :]).then_inc(s_dstrow, 16)
                sp.wait_ge(s_dstrow, 16)
                def load(g, b, prior, tail=0):
                    if prior is not None:
                        sp.wait_ge(s_T, prior)
                        sp.wait_ge(s_put, prior)
                    if tail:
                        sp.dma_start(xin[:, b, 0:tail - 1, D:2 * D], eh[g * GE:g * GE + (tail - 1) * P, :].rearrange("(j p) d -> p j d", p=P)).then_inc(s_eh[b], 16)
                        sp.dma_start(xin[0:TAIL_E, b, tail - 1, D:2 * D], eh[g * GE + (tail - 1) * P:E, :]).then_inc(s_eh[b], 16)
                    else:
                        sp.dma_start(xin[:, b, :, D:2 * D], eh[bass.ds(g * GE, GE), :].rearrange("(j p) d -> p j d", p=P)).then_inc(s_eh[b], 16)
                    rows = dst_rows.rearrange("(g j) p -> g (j p)", j=TPG)
                    sp.dma_start(dst_all[:, b, :], rows[bass.ds(g, 1), :].to_broadcast([P, GE])).then_inc(s_dstb[b], 16)

                for b in range(NB):
                    load(b, b, None)
                sp.wait_ge(s_xfirst[0], 16)
                sp.wait_ge(s_xfirst[1], 16)
                for c in range(LC - 1):
                    if c >= 2:
                        sp.wait_ge(s_two, c - 1)
                    sp.dma_start(node_chunk(c), x_chunk(c)).then_inc(s_xl[c % 2], 16)
                sp.wait_ge(s_lastz, 1)
                sp.wait_ge(s_two, LC - 2)
                move_last(sp, x, False, s_xl[(LC - 1) % 2])
                for c in range(LC - 1):
                    sp.wait_ge(s_two, c + 1)
                    sp.dma_start(sums[c * LN_BLOCKS * P:(c + 1) * LN_BLOCKS * P, :].rearrange("(b p) d -> p b d", p=P), node_chunk(c)).then_inc(s_init, 16)
                sp.wait_ge(s_two, LC)
                move_last(sp, sums, True, s_init)

                with sp.Fori(NB, G - NB, NB) as g0:
                    for b in range(NB):
                        load(g0 + b, b, g0 + (b - NB + 1))
                for b in range(NB):
                    g = G - NB + b
                    load(g, b, g - NB + 1, 0 if b < NB - 1 else FULL_T - (G - 1) * TPG + 1)
                sp.wait_ge(s_scq, 16 * T)
                for c in range(LC - 1):
                    sp.dma_start(node_chunk(c), sums[c * LN_BLOCKS * P:(c + 1) * LN_BLOCKS * P, :].rearrange("(b p) d -> p b d", p=P)).then_inc(s_back, 16)
                move_last(sp, sums, False, s_back)
                for c in range(LC - 1):
                    sp.wait_ge(s_norm, c + 1)
                    sp.dma_start(out[c * LN_BLOCKS * P:(c + 1) * LN_BLOCKS * P, :].rearrange("(b p) d -> p b d", p=P), node_chunk(c)).then_inc(s_out, 16)
                sp.wait_ge(s_norm, LC)
                move_last(sp, out, True, s_out)
                sp.wait_ge(s_out, 16 * (LC + 1))

        @block.gpsimd
        def _(pool):
            nc.gpsimd.memset(ident[:], 0.0).then_inc(s_const, 1)
            nc.gpsimd.memset(lower[:], 1.0).then_inc(s_const, 1)
            nc.gpsimd.memset(eps[:], 1e-5).then_inc(s_const, 1)
            nc.gpsimd.iota(spare[:], pattern=[[0, T]], base=N, channel_multiplier=1, allow_small_or_imprecise_dtypes=True).then_inc(s_const, 1)
            nc.gpsimd.iota(g_start[:], pattern=[[0, 1]], base=0, channel_multiplier=GE, allow_small_or_imprecise_dtypes=True).then_inc(s_const, 1)
            nc.gpsimd.iota(tile_start[:], pattern=[[P, TPG]], base=0, channel_multiplier=0, allow_small_or_imprecise_dtypes=True).then_inc(s_const, 1)
            nc.gpsimd.iota(tile_end[:], pattern=[[P, TPG]], base=TILE_SPAN * P, channel_multiplier=0, allow_small_or_imprecise_dtypes=True).then_inc(s_const, 1)
            nc.gpsimd.iota(win_at[:], pattern=[[P, WK]], base=0, channel_multiplier=1, allow_small_or_imprecise_dtypes=True).then_inc(s_near, 1)
            nc.gpsimd.iota(block_at[:], pattern=[[1, OHB * P]], base=0, channel_multiplier=0, allow_small_or_imprecise_dtypes=True).then_inc(s_near, 1)
            nc.gpsimd.memset(zeros[:], 0.0).then_inc(s_near, 1)
            nc.gpsimd.memset(half_neg[:], -0.5).then_inc(s_near, 1)
            nc.gpsimd.memset(nodes[:, G * CW:PAD_B * D], 0.0).then_inc(s_near, 1)
            nc.gpsimd.memset(junk[:], 0.0).then_inc(s_near, 1)
            pool.wait_ge(s_const, 7)
            nc.gpsimd.affine_select(out=ident[:], in_=ident[:], compare_op=ALU.not_equal, fill=1.0, base=0,
                                    pattern=[[-1, P]], channel_multiplier=1).then_inc(s_const, 1)
            nc.gpsimd.affine_select(out=lower[:], in_=lower[:], compare_op=ALU.is_gt, fill=0.0, base=0,
                                    pattern=[[-1, P]], channel_multiplier=1).then_inc(s_const, 1)

            counts = [pool.alloc_register(f"count{i}") for i in range(2 + TPG)]

            def held(i, value):
                if isinstance(value, int):
                    return value
                pool.reg_mov(counts[i], value)
                return counts[i]

            def settled():
                pool.wait_ge(s_const, 9)

            def gather(g, b, prior):
                turn = held(0, g + 1)
                prior = None if prior is None else held(1, prior)
                settled()
                pool.wait_ge(s_idxn, turn)
                if prior is not None:
                    pool.wait_ge(s_H, prior)
                for j in range(TPG):
                    nc.gpsimd.indirect_dma_start(out=xin[:, b, j, 0:D], out_offset=None, in_=x[:, :],
                                                 in_offset=bass.IndirectOffsetOnAxis(ap=idx_now[:, b, j:j + 1], axis=0)).then_inc(s_gath[b], 16)
                    nc.gpsimd.indirect_dma_start(out=hd[:, b, j, :], out_offset=None, in_=x[:, :],
                                                 in_offset=bass.IndirectOffsetOnAxis(ap=idx_now[:, b, TPG + j:TPG + j + 1], axis=0)).then_inc(s_gath[b], 16)

            def scatter(g, b, first):
                turn = held(0, g + 1)
                landed = [None if first and j == 0 else held(2 + j, g * (16 * TPG) + 16 * j) for j in range(TPG)]
                for j in range(TPG):
                    settled()
                    if j == 0:
                        pool.wait_ge(s_tot, turn)
                        pool.wait_ge(s_put, turn)
                    if landed[j] is not None:
                        pool.wait_ge(s_scq, landed[j])
                    nc.gpsimd.indirect_dma_start(out=sums[:, :], out_offset=bass.IndirectOffsetOnAxis(ap=put_at[:, b, j:j + 1], axis=0),
                                                 in_=tot[:, b, j, :], in_offset=None, compute_op=ALU.add).then_inc(s_scq, 16)

            def gather_src(g, b, fresh):
                turn = held(0, g + 1)
                prior = held(1, g - (NB - 1))
                settled()
                pool.wait_ge(s_srcn, turn)
                if not fresh:
                    pool.wait_ge(s_T, prior)
                for j in range(TPG):
                    nc.gpsimd.indirect_dma_start(out=hs[:, b, j, :], out_offset=None, in_=x[:, :],
                                                 in_offset=bass.IndirectOffsetOnAxis(ap=src_now[:, b, j:j + 1], axis=0)).then_inc(s_gath[b], 16)

            def inverse_std(c, b):
                pool.wait_ge(s_eps, c + 1)
                if not isinstance(c, int) or c >= 2:
                    pool.wait_ge(s_norm, c - 1)
                nc.gpsimd.tensor_tensor(inv_std[:, b, :], var_eps[:, b, :], half_neg[:, :], ALU.pow).then_inc(s_inv, 1)

            def rest_part(c, b):
                if not isinstance(c, int) or c >= PRE + 2:
                    pool.wait_ge(s_low, c - 1)
                pool.wait_ge(s_hi, c + 1)
                nc.gpsimd.tensor_tensor(x_rest[:, b, :, :], x_in[:, b, :, :], x_split[:, b, :, 0:D], ALU.subtract).then_inc(s_rest, 1)

            def near_step(i, b):
                if in_range(i, 2):
                    gather_src(i + 2, b, False)
                if in_range(i, PRE):
                    rest_part(i + PRE, b)
                if in_range(i, -5):
                    inverse_std(i - 5, (b + 1) % 2)

            pool.wait_ge(s_near, 9)
            pool.wait_ge(s_guard, 1)
            with pool.If(pool.value_load(near[0:1, 0:1], min_val=0, max_val=1)):
                for b in range(NB):
                    gather_src(b, b, True)
                for i in range(PEEL):
                    near_step(i, i % 2)
                with pool.Fori(PEEL, LOOP_END, 2) as i0:
                    for b in range(2):
                        near_step(i0 + b, b)
                for i in range(LOOP_END, G + 5):
                    near_step(i, i % 2)
            with pool.Else():
                for b in range(NB):
                    gather(b, b, None)
                pool.wait_ge(s_init, 16 * (LC + 1))
                for b in range(NB):
                    scatter(b, b, b == 0)
                    gather(b + NB, b, b + 1)
                with pool.Fori(NB, G - NB, NB) as g0:
                    for b in range(NB):
                        scatter(g0 + b, b, False)
                        gather(g0 + (b + NB), b, g0 + (b + 1))
                for b in range(NB):
                    scatter(G - NB + b, b, False)
                pool.wait_ge(s_scq, 16 * T)

        @block.tensor
        def _(pe):
            def turn_rows(bank, rows):
                for j in range(TPG):
                    mm = nc.tensor.transpose(bank[:, j * G:(j + 1) * G], rows[0:G, j, :], ident[0:G, 0:G])
                return mm

            pe.wait_ge(s_const, 9)
            pe.wait_ge(s_w, 16 * 11)
            nc.tensor.transpose(psA[0:D, 0:D], wue[:, :], ident[0:D, 0:D]).then_inc(s_wueT, 1)
            pe.wait_ge(s_wueTs, 1)
            nc.tensor.matmul(psB[0:D, 0:H], wueT[:, :], we1_low[:, :], start=True, stop=True).then_inc(s_fold, 1)
            pe.wait_ge(s_told, 1)
            for n, bank in enumerate((psT, psE, psS)):
                mm = nc.tensor.transpose(bank[0:1, 0:G], told[0:G, n:n + 1], ident[0:G, 0:G])
            mm.then_inc(s_rowT, 1)
            pe.wait_ge(s_rawf, 2)
            turn_rows(psC, rawf[:, 0, :, :]).then_inc(s_idxT, 1)
            turn_rows(psD, rawf[:, 1, :, :]).then_inc(s_idxT, 1)
            pe.wait_ge(s_inb, 1)
            turn_rows(psH, same[:, 1, :, :]).then_inc(s_inbT, 1)
            pe.wait_ge(s_we, 2)

            def transposes(g, b, round_, prior, tail=False):
                pe.wait_ge(s_eh[b], 16 * round_ + (16 if tail else 0))
                pe.wait_ge(s_gath[b], 16 * 2 * TPG * round_)
                for j in range(TPG):
                    mm = nc.tensor.transpose(psT[:, j * P:(j + 1) * P], xin[:, b, j, :], ident[:, :])
                mm.then_inc(s_T, 1)
                for j in range(TPG):
                    mm = nc.tensor.transpose(psH[0:D, j * P:(j + 1) * P], hd[:, b, j, :], ident[:, :])
                mm.then_inc(s_H, 1)

            def comb(g):
                pe.wait_ge(s_m12, g + 1)
                for j in range(TPG):
                    mm = nc.tensor.matmul(psE[:, j * D:(j + 1) * D], m12[:, j * P:(j + 1) * P], wc_wide[:, 0:D], start=True, stop=True)
                mm.then_inc(s_E, 1)

            def tile_sums(g, b, first=False):
                pe.wait_ge(s_same, g + 1)
                pe.wait_ge(s_msg, g + 1)
                if not first:
                    pe.wait_ge(s_tot, g)
                for j in range(TPG):
                    mm = nc.tensor.matmul(psS[:, j * D:(j + 1) * D], same[:, b, j, :], msg[:, j, :], start=True, stop=True)
                mm.then_inc(s_S, 1)

            def step(g, b, nxt_round, first=False, last=False, tail=False):
                pe.wait_ge(s_hsT, g + 1)
                nc.tensor.matmul(psA[:, :], w1_even[0:D, :], hsT[:, :], start=True, stop=True).then_inc(s_A, 1)
                if not first:
                    comb(g - 1)
                pe.wait_ge(s_ehT, g + 1)
                pe.wait_ge(s_prod, g + 1)
                nc.tensor.matmul(psC[:, :], we[:, :], peT[:, :], start=True, stop=True).then_inc(s_C, 1)
                if not first:
                    tile_sums(g - 1, (b + 1) % NB, first=isinstance(g, int) and g == 1)
                if not last:
                    transposes(g + 1, (b + 1) % NB, nxt_round, None, tail)
                pe.wait_ge(s_r1, g + 1)
                nc.tensor.matmul(psB[:, :], w2[:, :], r1[:, :], start=True, stop=True).then_inc(s_B, 1)
                pe.wait_ge(s_r2, g + 1)
                nc.tensor.matmul(psD[:, :], we2[:, :], r2[:, :], start=True, stop=True).then_inc(s_D, 1)

            def pick_hd(g, b, round_):
                pe.wait_ge(s_pick, g + 1)
                pe.wait_ge(s_win[b], round_ * 16)
                for j in range(TPG):
                    for k in range(WK):
                        for part in range(3):
                            mm = nc.tensor.matmul(psH[:, j * D:(j + 1) * D], pick[:, b, k, j * P:(j + 1) * P],
                                                  x_win[:, b, j + k, part * D:(part + 1) * D],
                                                  start=(k == 0 and part == 0), stop=(k == WK - 1 and part == 2))
                mm.then_inc(s_hd, 1)

            def turn_in(g, b):
                pe.wait_ge(s_prod, g + 1)
                for q in range(2):
                    nc.tensor.transpose(psH[:, (2 + q) * P:(3 + q) * P], hs[:, b, 2 * q:2 * q + 2, :].rearrange("p j d -> p (j d)"), ident[:, :])
                for j in range(TPG):
                    mm = nc.tensor.transpose(psT[:, j * P:(j + 1) * P], pe_in[:, b, j, :], ident[:, :])
                mm.then_inc(s_T, 1)

            def turn_out(g):
                pe.wait_ge(s_mlo, g + 1)
                rows = psE[:, 0:GE // 2].bitcast(F16)
                for j in range(TPG):
                    mm = nc.tensor.transpose(rows[:, j * P:(j + 1) * P], msgT_parts[:, j * P:(j + 1) * P], ident16[:, :])
                mm.then_inc(s_M, 1)

            def sum_messages(g, b):
                pe.wait_ge(s_putr, g + 1)
                pe.wait_ge(s_msgs, g + 1)
                if not isinstance(g, int) or g >= 1:
                    pe.wait_ge(s_add, g)
                for k in range(GB):
                    tiles = [j for j in range(TPG) if TILE_FIRST[j] <= k < TILE_END[j]]
                    for j in tiles:
                        rows = put[:, b, j, (k - TILE_FIRST[j]) * P:(k - TILE_FIRST[j] + 1) * P]
                        nc.tensor.matmul(psS[:, k * D:(k + 1) * D], rows, msg_parts[:, j, 0:D], start=(j == tiles[0]), stop=False)
                        mm = nc.tensor.matmul(psS[:, k * D:(k + 1) * D], rows, msg_parts[:, j, D:2 * D], start=False, stop=(j == tiles[-1]))
                mm.then_inc(s_agg, 1)

            def near_step(i, b, next_round, edge_count):
                pe.wait_ge(s_hsP, i + 1)
                pairs = psA[:, :].rearrange("p (q r e) -> p q r e", q=2, r=2)
                cols = hsP[:, :].rearrange("p (q e) -> p q e", q=2)
                nc.tensor.matmul(pairs[:, :, 0, :], w1_even[:, :], cols, start=True, stop=True)
                nc.tensor.matmul(pairs[:, :, 1, :], w1_odd[:, :], cols, start=True, stop=True).then_inc(s_A, 1)
                pe.wait_ge(s_ehT, i + 1)
                nc.tensor.matmul(psC[:, :], we[:, :], peT[:, :], start=True, stop=True).then_inc(s_C, 1)
                if in_range(i, 1):
                    pick_hd(i + 1, (b + 1) % NB, next_round)
                if in_range(i, -1):
                    turn_out(i - 1)
                pe.wait_ge(s_r1, i + 1)
                nc.tensor.matmul(psB[:, :], w2[:, :], r1[:, :], start=True, stop=True).then_inc(s_B, 1)
                pe.wait_ge(s_r2, i + 1)
                nc.tensor.matmul(psD[:, :], we2[:, :], r2[:, :], start=True, stop=True).then_inc(s_D, 1)
                if in_range(i, -1):
                    sum_messages(i - 1, (b + 1) % NB)
                if in_range(i, 1):
                    pe.wait_ge(s_eh[(b + 1) % NB], edge_count)
                    turn_in(i + 1, (b + 1) % NB)
                pe.wait_ge(s_m12, i + 1)
                nc.tensor.matmul(psE[:, :], wc_wide[:, :], m12[:, :], start=True, stop=True).then_inc(s_E, 1)

            pe.wait_ge(s_near, 9)
            pe.wait_ge(s_guard, 1)
            with pe.If(pe.value_load(near[0:1, 0:1], min_val=0, max_val=1)):
                pe.wait_ge(s_idx, 1)
                pe.wait_ge(s_dinb, 1)
                pick_hd(0, 0, 1)
                pe.wait_ge(s_eh[0], 16)
                turn_in(0, 0)
                near_step(0, 0, 1, 16)
                near_step(1, 1, 2, 32)
                with pe.Fori(1, G // 2 - 1) as k:
                    near_step(k * 2, 0, k + 1, k * 16 + 16)
                    near_step(k * 2 + 1, 1, k + 2, k * 16 + 32)
                near_step(G - 2, 0, G // 2, 16 * (G // 2) + 16)
                near_step(G - 1, 1, None, None)
                turn_out(G - 1)
                sum_messages(G - 1, 1)
            with pe.Else():
                pe.wait_ge(s_idx, 3)
                pe.wait_ge(s_dinb, 1)
                transposes(0, 0, 1, None)
                step(0, 0, 1, first=True)
                step(1, 1, 2)
                with pe.Fori(1, G // NB - 1) as k:
                    step(k * NB, 0, k + 1)
                    step(k * NB + 1, 1, k + 2)
                step(G - 2, 0, G // NB, tail=True)
                step(G - 1, 1, None, last=True)
                comb(G - 1)
                tile_sums(G - 1, 1)

        @block.scalar
        def _(act):
            act.wait_ge(s_raw[1], 16 * 2)
            for n in range(2):
                half = slice(n * (PRE // 2), (n + 1) * (PRE // 2))
                act.dma_start(nodes[:, half.start * CW:half.stop * CW].rearrange("p (b d) -> p b d", d=D),
                              x[half.start * GE:half.stop * GE, :].rearrange("(b p) d -> p b d", p=P)).then_inc(s_xfirst[n], 16)
            for n in range(2):
                act.wait_ge(s_xfirst[n], 16)
                nc.scalar.activation(x_split_first[:, n, :, 0:D], first_x(n), ACT.Copy).then_inc(s_hi, PRE // 2)
            act.wait_ge(s_near, 9)
            for first in [n * P for n in range(FRONT)] + [(FRONT + n) * P + G * GE for n in range(BACK)]:
                act.dma_start(x_parts[first:first + P, :], zeros[:, :]).then_inc(s_xpad, 16)
            act.wait_ge(s_wueT, 1)
            nc.scalar.activation(wueT[:, :], psA[0:D, 0:D], ACT.Copy).then_inc(s_wueTs, 1)
            act.wait_ge(s_fold, 1)
            nc.scalar.activation(we[0:D, :], psB[0:D, 0:H], ACT.Copy, scale=0.2).then_inc(s_we, 1)
            act.wait_ge(s_w, 16 * 11)
            nc.scalar.activation(we[D:P, :], we[D:P, :], ACT.Copy, scale=0.8).then_inc(s_we, 1)

            def evacuate(g):
                act.wait_ge(s_T, g + 1)
                nc.scalar.activation(hsT[:, :], psT[0:D, :], ACT.Copy).then_inc(s_hsT, 1)
                nc.scalar.activation(peT[D:P, :], psT[D:P, :], ACT.Copy).then_inc(s_ehT, 1)

            def tanh(g):
                act.wait_ge(s_E, g + 1)
                nc.scalar.activation(msg[:, :, :].rearrange("p j d -> p (j d)"), psE[:, 0:TPG * D], ACT.Tanh).then_inc(s_msg, 1)

            def step(g, first=False, last=False):
                act.wait_ge(s_A, g + 1)
                nc.scalar.activation(r1[:, :], psA[:, :], ACT.Relu, bias=b1[:, 0:1]).then_inc(s_r1, 1)
                if not first:
                    tanh(g - 1)
                act.wait_ge(s_C, g + 1)
                nc.scalar.activation(r2[:, :], psC[:, :], ACT.Relu, bias=be1[:, 0:1]).then_inc(s_r2, 1)
                if not last:
                    evacuate(g + 1)
                act.wait_ge(s_B, g + 1)
                nc.scalar.activation(m1[:, :], psB[:, :], ACT.Copy).then_inc(s_m1, 1)


            for n in range(2):
                act.wait_ge(s_rest, (n + 1) * (PRE // 2))
                nc.scalar.activation(x_split_first[:, n, :, D:2 * D], first_rest(n), ACT.Copy).then_inc(s_mid, PRE // 2)

            def src_copy(g, b, gathers):
                if gathers is not None:
                    act.wait_ge(s_gath[b], gathers)
                nc.scalar.activation(src_now[:, b, :].rearrange("p (a j) -> p a j", a=1), idx[:, bass.ds(g, 1), 0:TPG], ACT.Copy).then_inc(s_srcn, 1)

            def high_part(c, b, loads, stores):
                act.wait_ge(s_xin[b], loads)
                if stores is not None:
                    act.wait_ge(s_xst[b], stores)
                nc.scalar.activation(x_split[:, b, :, 0:D], x_in[:, b, :, :], ACT.Copy).then_inc(s_hi, 1)
                nc.scalar.activation(nodes[:, bass.ds(c * CW, CW)], x_in[:, b, :, :].rearrange("p b d -> p (b d)"), ACT.Copy, scale=2.0).then_inc(s_two, 1)

            def middle_part(c, b):
                act.wait_ge(s_rest, c + 1)
                nc.scalar.activation(x_split[:, b, :, D:2 * D], x_rest[:, b, :, :], ACT.Copy).then_inc(s_mid, 1)

            def copy_in(g):
                act.wait_ge(s_T, g + 1)
                nc.scalar.activation(hsP[:, :], psH[:, 2 * P:4 * P], ACT.Copy).then_inc(s_hsP, 1)
                nc.scalar.activation(peT[:, :], psT[:, :], ACT.Copy).then_inc(s_ehT, 1)

            def near_tanh(g):
                act.wait_ge(s_E, g + 1)
                nc.scalar.activation(msgT, psE[:, :], ACT.Tanh).then_inc(s_tanh, 1)
                act.wait_ge(s_tanh, g + 1)
                nc.scalar.activation(msgT_parts[:, :], msgT, ACT.Copy, scale=SCALE).then_inc(s_mhi, 1)

            def copy_messages(g):
                act.wait_ge(s_M, g + 1)
                nc.scalar.activation(msg_parts[:, :, :].rearrange("p j d -> p (j d)"), psE[:, 0:GE // 2].bitcast(F16), ACT.Copy).then_inc(s_msgs, 1)

            def add_eps(c, b):
                act.wait_ge(s_mv, c + 1)
                nc.scalar.activation(var_eps[:, b, :], mv[:, b, :, 1], ACT.Relu, bias=eps[:, 0:1]).then_inc(s_eps, 1)

            def load_edges(g, b):
                if isinstance(g, int) and g == G - 1:
                    tail = FULL_T - g * TPG + 1
                    act.dma_start(pe_in[:, b, 0:tail - 1, D:2 * D], eh[g * GE:g * GE + (tail - 1) * P, :].rearrange("(j p) d -> p j d", p=P)).then_inc(s_eh[b], 16)
                    act.dma_start(pe_in[0:TAIL_E, b, tail - 1, D:2 * D], eh[g * GE + (tail - 1) * P:E, :]).then_inc(s_eh[b], 16)
                else:
                    act.dma_start(pe_in[:, b, :, D:2 * D], eh[bass.ds(g * GE, GE), :].rearrange("(j p) d -> p j d", p=P)).then_inc(s_eh[b], 16)

            def near_step(i, b, half):
                act.wait_ge(s_A, i + 1)
                nc.scalar.activation(r1[:, :], psA[:, :], ACT.Relu, bias=b1[:, 0:1]).then_inc(s_r1, 1)
                act.wait_ge(s_C, i + 1)
                nc.scalar.activation(r2[:, :], psC[:, :], ACT.Relu, bias=be1[:, 0:1]).then_inc(s_r2, 1)
                if in_range(i, -1):
                    copy_messages(i - 1)
                act.wait_ge(s_B, i + 1)
                nc.scalar.activation(m1[:, :], psB[:, :], ACT.Copy).then_inc(s_m1, 1)
                if in_range(i, 3):
                    src_copy(i + 3, (b + 1) % 2, (half + 1 + b) * (16 * TPG))
                if in_range(i, PRE):
                    loads = half * 16 + 16
                    if isinstance(i, int) and i + PRE == G - 1:
                        loads = loads + 16
                    high_part(i + PRE, b, loads, None if isinstance(i, int) and i < 2 else half * 16)
                if in_range(i, PRE - 1) and not (isinstance(i, int) and i < 1):
                    middle_part(i + (PRE - 1), (b + 1) % 2)
                if in_range(i, -5):
                    add_eps(i - 5, (b + 1) % 2)
                if in_range(i, 1):
                    copy_in(i + 1)
                if in_range(i, 3):
                    load_edges(i + 3, (b + 1) % 2)
                near_tanh(i)

            act.wait_ge(s_idx, 1)
            act.wait_ge(s_guard, 1)
            with act.If(act.value_load(near[0:1, 0:1], min_val=0, max_val=1)):
                for b in range(NB):
                    src_copy(b, b, None)
                    load_edges(b, b)
                for n in range(2):
                    act.wait_ge(s_rest, (n + 1) * (PRE // 2))
                    nc.scalar.activation(first_x(n), first_x(n), ACT.Copy, scale=2.0).then_inc(s_two, PRE // 2)
                copy_in(0)
                load_edges(2, 0)
                src_copy(2, 0, 16 * TPG)
                for i in range(ACT_PEEL):
                    near_step(i, i % 2, i // 2)
                with act.Fori(ACT_PEEL // 2, LOOP_END // 2) as k:
                    for b in range(2):
                        near_step(k * 2 + b, b, k)
                for i in range(LOOP_END, G):
                    near_step(i, i % 2, i // 2)
                copy_messages(G - 1)
                for c in range(G - 5, G):
                    add_eps(c, c % 2)
            with act.Else():
                for c in range(LC):
                    act.wait_ge(s_xl[c % 2], 16 * (c // 2 + 1) + (16 if c == LC - 1 else 0))
                    nc.scalar.activation(nodes[:, c * LW:(c + 1) * LW], nodes[:, c * LW:(c + 1) * LW], ACT.Copy, scale=2.0).then_inc(s_two, 1)
                evacuate(0)
                step(0, first=True)
                with act.Fori(1, G - 1) as g:
                    step(g)
                step(G - 1, last=True)
                tanh(G - 1)
                for c in range(LC + 1):
                    if c < LC:
                        act.wait_ge(s_cent, c + 1)
                        if c >= 2:
                            act.wait_ge(s_ssq, c - 1)
                        nc.scalar.activation(sq[:, c % 2, :], nodes[:, c * LW:(c + 1) * LW], ACT.Square).then_inc(s_sq, 1)
                    if c >= 1:
                        act.wait_ge(s_ssq, c)
                        nc.scalar.activation(std[:, (c - 1) % 2, :], ssq[:, (c - 1) % 2, :], ACT.Sqrt, bias=eps[:, 0:1], scale=1.0 / D).then_inc(s_std, 1)

        @block.vector
        def _(dve):
            pad = (E - (G - 1) * GE) // P
            nc.vector.memset(raw[:, 1, pad:TPG, :], N).then_inc(s_pad, 1)
            nc.vector.memset(raw[:, 0, pad:TPG, :], 0).then_inc(s_pad, 1)
            nc.vector.memset(nodes[:, (B - 1) * D:B * D], 0.0).then_inc(s_lastz, 1)
            nc.vector.memset(w1_even[D:P, :], 0.0).then_inc(s_near, 1)
            nc.vector.memset(w1_odd[0:D, :], 0.0).then_inc(s_near, 1)
            steps = [0]

            def step_row(*ins):
                for i in ins:
                    steps[0] += 1
                    i.then_inc(s_row, 1)
                dve.wait_ge(s_row, steps[0])

            def less(out_, a, b):
                return nc.vector.tensor_tensor(out_, a, b, ALU.subtract)

            dve.wait_ge(s_raw[1], 16 * 2)
            nc.vector.tensor_copy(rawf[0:G, 1, :, :], raw[0:G, 1, :, :]).then_inc(s_rawf, 1)
            dve.wait_ge(s_rawf, 1)
            dve.wait_ge(s_const, 9)
            nc.vector.tensor_copy(ident16[:, :], ident[:, :]).then_inc(s_near, 1)
            step_row(nc.vector.tensor_reduce(row_min[0:G, :], rawf[0:G, 1, :, :], AX_X, ALU.min),
                     nc.vector.tensor_scalar(same[0:G, 0, :, :], rawf[0:G, 1, :, :], float(N - 1), None, ALU.min),
                     nc.vector.tensor_scalar(tile_first[0:G, :], tile_end[0:G, :], float((TILE_SPAN + 1) * P), 0.0, ALU.subtract, ALU.max))
            step_row(nc.vector.tensor_reduce(row_max[0:G, :], same[0:G, 0, :, :], AX_X, ALU.max),
                     nc.vector.tensor_copy(row_mini[0:G, :], row_min[0:G, :]),
                     less(row_rel[0:G, 0, :], row_min[0:G, :], tile_start[0:G, :]))
            step_row(nc.vector.tensor_scalar(row_alii[0:G, :], row_mini[0:G, :], (1 << 20) - P, None, ALU.bitwise_and),
                     nc.vector.tensor_reduce(low[0:G, :], row_rel[0:G, 0, :], AX_X, ALU.min),
                     less(row_rel[0:G, 2, :], row_max[0:G, :], tile_start[0:G, :]),
                     less(row_rel[0:G, 3, :], row_max[0:G, :], tile_end[0:G, :]))
            step_row(less(row_rel[0:G, 1, :], row_alii[0:G, :], tile_first[0:G, :]),
                     nc.vector.tensor_scalar(g_base[0:G, :], low[0:G, :], float(-FRONT * P), float((BACK - GW) * P + G * GE), ALU.max, ALU.min),
                     nc.vector.tensor_reduce(row_last[0:G, :], row_rel[0:G, 2:4, :], AX_X, ALU.max))
            step_row(nc.vector.tensor_reduce(g_ali[0:G, :], row_rel[0:G, 1, :], AX_X, ALU.min),
                     nc.vector.tensor_scalar(row_base[0:G, :], tile_start[0:G, :], g_base[0:G, :], None, ALU.add),
                     nc.vector.tensor_scalar(excess[0:G, 0:1], row_last[0:G, 0:1], g_base[0:G, :], float(WIN - 1), ALU.subtract, ALU.subtract),
                     less(excess[0:G, 1:2], g_base[0:G, :], low[0:G, :]),
                     nc.vector.tensor_scalar(told[0:G, 0:1], g_base[0:G, :], float(FRONT * P), None, ALU.add))
            step_row(nc.vector.tensor_scalar(excess[0:G, 2:3], row_last[0:G, 1:2], g_ali[0:G, :], 1.0, ALU.subtract, ALU.add),
                     nc.vector.tensor_scalar(excess[0:G, 3:4], g_ali[0:G, :], -1.0, None, ALU.mult),
                     nc.vector.tensor_scalar(excess[0:G, 4:5], g_ali[0:G, :], g_start[0:G, :], float(NEAR * P), ALU.subtract, ALU.subtract),
                     nc.vector.tensor_scalar(excess[0:G, 5:6], g_start[0:G, :], g_ali[0:G, :], float(NEAR * P), ALU.subtract, ALU.subtract),
                     nc.vector.tensor_scalar(row_first[0:G, :], tile_first[0:G, :], g_ali[0:G, :], None, ALU.add),
                     nc.vector.tensor_scalar(told[0:G, 1:2], g_ali[0:G, :], float(D) / P, None, ALU.mult))
            nc.vector.tensor_reduce(told[0:G, 2:3], excess[0:G, :], AX_X, ALU.max).then_inc(s_told, 1)
            for j in range(TPG):
                i = nc.vector.tensor_scalar(row_loc[0:G, j, :], rawf[0:G, 1, j, :], row_base[0:G, j:j + 1], 1000.0, ALU.subtract, ALU.min)
            i.then_inc(s_rowv, 1)
            for j in range(TPG):
                i = nc.vector.tensor_scalar(same[0:G, 1, j, :], rawf[0:G, 1, j, :], row_first[0:G, j:j + 1], None, ALU.subtract)
            i.then_inc(s_inb, 1)
            dve.wait_ge(s_raw[0], 16 * 2)
            nc.vector.tensor_copy(rawf[0:G, 0, :, :], raw[0:G, 0, :, :]).then_inc(s_rawf, 1)
            for n in range(2):
                dve.wait_ge(s_hi, (n + 1) * (PRE // 2))
                nc.vector.tensor_tensor(first_rest(n), first_x(n), x_split_first[:, n, :, 0:D], ALU.subtract).then_inc(s_rest, PRE // 2)
            dve.wait_ge(s_rowT, 1)
            step_row(nc.vector.tensor_reduce(most[:, :], psS[0:1, 0:G], AX_X, ALU.max),
                     nc.vector.tensor_copy(g_base_i[:, :], psT[0:1, 0:G]),
                     nc.vector.tensor_copy(g_col_i[:, :], psE[0:1, 0:G]))
            nc.vector.tensor_scalar(near[:, :], most[:, :], 0.0, None, ALU.is_le).then_inc(s_guard, 1)

            def by_group(cols):
                return cols.rearrange("p (g j) -> p j g", j=TPG)

            def by_tile(bank):
                return bank[:, 0:T].rearrange("p (j g) -> p j g", j=TPG)

            dve.wait_ge(s_idxT, 1)
            nc.vector.tensor_copy(idx[:, :, 0:TPG].rearrange("p g j -> p j g"), by_tile(psC)).then_inc(s_idx, 1)
            dve.wait_ge(s_inbT, 1)
            nc.vector.tensor_copy(by_group(dst_in_block[:, :]), by_tile(psH)).then_inc(s_dinb, 1)
            dve.wait_ge(s_dinb, 1)
            dve.wait_ge(s_near, 9)

            def make_pick(g, b, round_):
                dve.wait_ge(s_dwin[b], round_ * 16)
                if not isinstance(g, int) or g >= NB:
                    dve.wait_ge(s_hd, g - (NB - 1))
                for k in range(WK):
                    i = nc.vector.tensor_scalar(pick[:, b, k, :], dst_win[:, b, :], win_at[:, k:k + 1], None, ALU.is_equal)
                i.then_inc(s_pick, 1)

            def make_put(g, b):
                if not isinstance(g, int) or g >= NB:
                    dve.wait_ge(s_agg, g - (NB - 1))
                for j in range(TPG):
                    wide = (TILE_END[j] - TILE_FIRST[j]) * P
                    i = nc.vector.tensor_scalar(put[:, b, j, 0:wide], block_at[:, 0:wide], dst_in_block[:, bass.ds(g * TPG + j, 1)], None, ALU.is_equal)
                i.then_inc(s_putr, 1)

            def near_product(g, b, gathers):
                dve.wait_ge(s_gath[b], gathers)
                dve.wait_ge(s_hd, g + 1)
                nc.vector.tensor_tensor(pe_in[:, b, :, 0:D], psH[:, 0:TPG * D].rearrange("p (j d) -> p j d", d=D), hs[:, b, :, :], ALU.mult).then_inc(s_prod, 1)

            def low_message(g):
                dve.wait_ge(s_mhi, g + 1)
                nc.vector.scalar_tensor_tensor(out=msgT_parts[D:P, :], in0=msgT[D:P, :], scalar=SCALE, in1=msgT_parts[D:P, :],
                                               op0=ALU.mult, op1=ALU.subtract).then_inc(s_mlo, 1)

            def first_column(g):
                return dve.value_load(g_col_i[0:1, bass.ds(g, 1)], min_val=0, max_val=(B - 1) * D)

            def add_sums(g, col, chunks):
                dve.wait_ge(s_agg, g + 1)
                dve.wait_ge(s_two, chunks)
                nc.vector.scalar_tensor_tensor(out=nodes[:, bass.ds(col, GB * D)], in0=psS[:, 0:GB * D], scalar=1.0 / SCALE,
                                               in1=nodes[:, bass.ds(col, GB * D)], op0=ALU.mult, op1=ALU.add).then_inc(s_add, 1)

            def low_part(c, b):
                dve.wait_ge(s_mid, c + 1)
                nc.vector.tensor_tensor(x_split[:, b, :, 2 * D:3 * D], x_rest[:, b, :, :], x_split[:, b, :, D:2 * D], ALU.subtract).then_inc(s_low, 1)

            def chunk_stats(c, b):
                for k in range(CB):
                    i = nc.vector.bn_stats(stats[:, b, k, :], nodes[:, bass.ds(c * CW + k * D, D)])
                i.then_inc(s_stats, 1)

            def chunk_mean_var(c, b):
                for k in range(CB):
                    i = nc.vector.bn_aggr(mv[:, b, k, :], stats[:, b, k, :])
                i.then_inc(s_mv, 1)

            def normalise(c, b):
                dve.wait_ge(s_inv, c + 1)
                for k in range(CB):
                    here = nodes[:, bass.ds(c * CW + k * D, D)]
                    i = nc.vector.tensor_scalar(here, here, mv[:, b, k, 0:1], inv_std[:, b, k:k + 1], ALU.subtract, ALU.mult)
                i.then_inc(s_norm, 1)

            def near_step(i, b, half):
                o = (b + 1) % 2
                if in_range(i, -1):
                    low_message(i - 1)
                if in_range(i, 2):
                    make_pick(i + 2, b, half + 2)
                if in_range(i, 0):
                    make_put(i, b)
                if in_range(i, 1):
                    near_product(i + 1, o, (half + 1 + b) * (16 * TPG))
                if in_range(i, -6):
                    normalise(i - 6, b)
                if in_range(i, 0):
                    dve.wait_ge(s_D, i + 1)
                    dve.wait_ge(s_m1, i + 1)
                    nc.vector.tensor_tensor(m12[:, :], psD[:, :], m1[:, :], ALU.mult).then_inc(s_m12, 1)
                if in_range(i, -1):
                    col = first_column(i - 1)
                if in_range(i, -4):
                    dve.wait_ge(s_stats, i - 3)
                    if in_range(i, -6):
                        dve.wait_ge(s_norm, i - 5)
                if in_range(i, PRE - 1) and not (isinstance(i, int) and i < 1):
                    low_part(i + (PRE - 1), o)
                if in_range(i, -4):
                    chunk_mean_var(i - 4, b)
                if in_range(i, -1):
                    add_sums(i - 1, col, min(i + 3, G) if isinstance(i, int) else i + 3)
                if in_range(i, -1):
                    dve.wait_ge(s_add, i)
                if in_range(i, -3):
                    chunk_stats(i - 3, o)

            with dve.If(dve.value_load(near[0:1, 0:1], min_val=0, max_val=1)):
                for n in range(2):
                    dve.wait_ge(s_mid, (n + 1) * (PRE // 2))
                    nc.vector.tensor_tensor(x_split_first[:, n, :, 2 * D:3 * D], first_rest(n), x_split_first[:, n, :, D:2 * D], ALU.subtract).then_inc(s_low, PRE // 2)
                for b in range(NB):
                    make_pick(b, b, 1)
                near_product(0, 0, 16 * TPG)
                for i in range(PEEL):
                    near_step(i, i % 2, i // 2)
                with dve.Fori(PEEL // 2, LOOP_END // 2) as k:
                    for b in range(2):
                        near_step(k * 2 + b, b, k)
                for i in range(LOOP_END, G + 6):
                    near_step(i, i % 2, i // 2)

            def indices(g, b, prior):
                if prior is not None:
                    dve.wait_ge(s_gath[b], prior)
                nc.vector.tensor_copy(idx_now[:, b, :].rearrange("p (a j) -> p a j", a=1), idx[:, bass.ds(g, 1), :]).then_inc(s_idxn, 1)

            def product(g):
                dve.wait_ge(s_H, g + 1)
                dve.wait_ge(s_hsT, g + 1)
                nc.vector.tensor_tensor(peT[0:D, :], psH[0:D, :], hsT[:, :], ALU.mult).then_inc(s_prod, 1)

            VC = 3

            def equal_dst(g, b, round_, prior):
                dve.wait_ge(s_dstb[b], 16 * round_)
                for j in range(TPG):
                    i = nc.vector.tensor_scalar(same[:, b, j, :], dst_all[:, b, j * P:(j + 1) * P],
                                            dstf[:, bass.ds(g * TPG + j, 1)], None, ALU.is_equal)
                i.then_inc(s_same, 1)
                dve.wait_ge(s_same, g + 1)
                for j in range(TPG):
                    i = nc.vector.tensor_tensor_reduce(junk[:, j, :], same[:, b, j, :], lower[:, :], 1.0, 0.0, ALU.mult, ALU.add, earlier[:, j:j + 1])
                i.then_inc(s_v, 1)
                dve.wait_ge(s_v, g * VC + (V0 + 1))
                nc.vector.tensor_scalar(dup[:, :], earlier[:, :], 1.0, None, ALU.min).then_inc(s_v, 1)
                dve.wait_ge(s_v, g * VC + (V0 + 2))
                nc.vector.tensor_tensor(moved[:, :], dup[:, :], spare[:, bass.ds(g * TPG, TPG)], ALU.mult).then_inc(s_v, 1)
                dve.wait_ge(s_v, g * VC + (V0 + 3))
                if prior is not None:
                    dve.wait_ge(s_scq, prior * (16 * TPG))
                nc.vector.tensor_tensor(put_at[:, b, :], moved[:, :], dstf[:, bass.ds(g * TPG, TPG)], ALU.add).then_inc(s_put, 1)

            def totals(g, b, prior):
                dve.wait_ge(s_S, g + 1)
                if prior is not None:
                    dve.wait_ge(s_scq, prior * (16 * TPG))
                nc.vector.tensor_copy(tot[:, b, :, :].rearrange("p j d -> p (j d)"), psS[:, 0:TPG * D]).then_inc(s_tot, 1)

            def step(g, b, round_, first=False, last=False, peeled=False):
                pr = None if peeled else g - (NB - 1)
                if not last:
                    indices(g + NB, b, round_ * (16 * 2 * TPG))
                equal_dst(g, b, round_, pr)
                if not first:
                    totals(g - 1, (b + 1) % NB, None if peeled else g - NB)
                product(g + 1)
                dve.wait_ge(s_D, g + 1)
                dve.wait_ge(s_m1, g + 1)
                nc.vector.tensor_tensor(m12[:, :], psD[:, :], m1[:, :], ALU.mult).then_inc(s_m12, 1)

            def step_end(g, b, round_, more):
                equal_dst(g, b, round_, g - (NB - 1))
                totals(g - 1, (b + 1) % NB, g - NB)
                if more:
                    product(g + 1)
                dve.wait_ge(s_D, g + 1)
                dve.wait_ge(s_m1, g + 1)
                nc.vector.tensor_tensor(m12[:, :], psD[:, :], m1[:, :], ALU.mult).then_inc(s_m12, 1)

            V0 = 1
            with dve.Else():
                dve.wait_ge(s_idxT, 2)
                nc.vector.tensor_scalar(idx[:, :, TPG:2 * TPG].rearrange("p g j -> p j g"), by_tile(psD), float(N - 1), None, ALU.min).then_inc(s_idx, 1)
                nc.vector.tensor_copy(by_group(dstf[:, :]), by_tile(psD)).then_inc(s_idx, 1)
                dve.wait_ge(s_idx, 3)
                nc.vector.tensor_tensor(spare[:, :], spare[:, :], dstf[:, :], ALU.subtract).then_inc(s_v, 1)
                dve.wait_ge(s_v, 1)
                for b in range(NB):
                    indices(b, b, None)
                product(0)
                step(0, 0, 1, first=True, peeled=True)
                step(1, 1, 1, peeled=True)
                with dve.Fori(1, G // NB - 1) as k:
                    step(k * NB, 0, k + 1)
                    step(k * NB + 1, 1, k + 1)
                step_end(G - 2, 0, G // NB, True)
                step_end(G - 1, 1, G // NB, False)
                totals(G - 1, 1, G - NB)

                dve.wait_ge(s_back, 16 * (LC + 1))
                def scale_out(c):
                    dve.wait_ge(s_std, c + 1)
                    nc.vector.reciprocal(rstd[:, c % 2, :], std[:, c % 2, :]).then_inc(s_ln, 1)
                    ln[0] += 1
                    dve.wait_ge(s_ln, ln[0])
                    nc.vector.tensor_tensor(node_chunk(c), node_chunk(c), rstd[:, c % 2, :].rearrange("p (b a) -> p b a", a=1).to_broadcast([P, LN_BLOCKS, D]), ALU.mult).then_inc(s_norm, 1)

                ln = [0]
                for c in range(LC + 1):
                    if c < LC:
                        nc.vector.tensor_reduce(mean[:, c % 2, :], node_chunk(c), AX_X, ALU.add).then_inc(s_ln, 1)
                        ln[0] += 1
                        dve.wait_ge(s_ln, ln[0])
                        nc.vector.tensor_scalar(nmean[:, c % 2, :], mean[:, c % 2, :], 1.0 / D, None, ALU.mult).then_inc(s_ln, 1)
                        ln[0] += 1
                        dve.wait_ge(s_ln, ln[0])
                        nc.vector.tensor_tensor(node_chunk(c), node_chunk(c), nmean[:, c % 2, :].rearrange("p (b a) -> p b a", a=1).to_broadcast([P, LN_BLOCKS, D]), ALU.subtract).then_inc(s_cent, 1)
                    if c >= 1:
                        scale_out(c - 1)
                    if c < LC:
                        dve.wait_ge(s_sq, c + 1)
                        if c >= 2:
                            dve.wait_ge(s_std, c - 1)
                        nc.vector.tensor_reduce(ssq[:, c % 2, :], sq[:, c % 2, :].rearrange("p (b d) -> p b d", d=D), AX_X, ALU.add).then_inc(s_ssq, 1)


_INS = ['x', 'src', 'dst', 'edge_attr_64', 'L0_gnn_W_node1', 'L0_gnn_b_node1', 'L0_gnn_W_node2', 'L0_gnn_W_edge1',
        'L0_gnn_b_edge1', 'L0_gnn_W_edge2', 'L0_gnn_W_comb', 'L0_gnn_W_ue']


def kernel(**inputs):
    import numpy as _np
    import concourse.bacc as _bacc
    from concourse import mybir as _mybir
    from concourse.bass_utils import run_bass_kernel_spmd as _run

    nc = _bacc.Bacc("TRN2", target_bir_lowering=False, num_devices=1)
    arrays, args = {}, []
    for name in _INS:
        a = _np.ascontiguousarray(inputs[name])
        arrays[f"in_{name}_dram"] = a
        args.append(nc.dram_tensor(f"in_{name}_dram", a.shape, _mybir.dt.from_np(a.dtype), kind="ExternalInput").ap())
    args.append(nc.dram_tensor("out_dram", (50000, 64), _mybir.dt.float32, kind="ExternalOutput").ap())
    gnn_kernel(nc, *args)
    r = _run(nc, [arrays], core_ids=[0])
    return r.results[0]["out_dram"]
```
